# Optimizing a Trainium2 kernel written in Bass

```python
import numpy as np
import jax
import jax.numpy as jnp

def _softmax(x, axis=-1):
    return jax.nn.softmax(x, axis=axis)

def _gelu(x):
    return jax.nn.gelu(x, approximate=True)

def _silu(x):
    return jax.nn.silu(x)

def _sigmoid(x):
    return jax.nn.sigmoid(x)

def _layernorm(x, axis=-1, eps=1e-05):
    m = jnp.mean(x, axis=axis, keepdims=True)
    v = jnp.var(x, axis=axis, keepdims=True)
    return (x - m) / jnp.sqrt(v + eps)

def _scatter_add(tgt, idx, src, axis=0):
    return tgt.at[idx].add(src)

def _segment_sum(src, seg, n):
    return jax.ops.segment_sum(src, seg, n)
kernel_name = 'mk_gnn_preln_d2_gnn_r32_7553ad'

def setup_inputs(seed: int=0):
    np.random.seed(seed)
    _w = jnp.asarray

    def _rec_inputs():
        import jax
        import jax.numpy as jnp
        _gk = jax.random.key(seed)
        x = -0.0005121 + 1.001 * jax.random.normal(jax.random.fold_in(_gk, 1), (50000, 64), jnp.float32)
        src = jax.random.randint(jax.random.fold_in(_gk, 2), (50000,), 0, 50000, jnp.int32)
        dst = jnp.minimum((50000 * jax.random.uniform(jax.random.fold_in(_gk, 3), (50000,)) ** 2.0).astype(jnp.int32), 49999)
        _o = jnp.argsort(dst, stable=True)
        src = src[_o]
        dst = dst[_o]
        edge_type_32 = jax.random.randint(jax.random.fold_in(_gk, 13), (50000,), 0, 32, jnp.int32)
        return (x, src, dst, edge_type_32)
    x, src, dst, edge_type_32 = _rec_inputs()

    def _L0_gnn_setup():
        import jax, jax.numpy as jnp
        import numpy as np
        N, E, D = (50000, 25000, 64)
        key = jax.random.key(seed)
        ks = jax.random.split(key, 8)
        s = 1.0 / np.sqrt(2 * D)
        inp = {'node_emb': jax.random.normal(ks[0], (N, D), dtype=jnp.float32), 'edge_index': jax.random.randint(ks[1], (2, E), 0, N, dtype=jnp.int64), 'W1': jax.random.normal(ks[2], (2 * D, D), dtype=jnp.float32) * s, 'b1': jnp.zeros((D,), dtype=jnp.float32), 'W2': jax.random.normal(ks[3], (D, D), dtype=jnp.float32) * (1.0 / np.sqrt(D)), 'b2': jnp.zeros((D,), dtype=jnp.float32), 'Wg': jax.random.normal(ks[4], (D, D), dtype=jnp.float32) * (1.0 / np.sqrt(D)), 'bg': jnp.zeros((D,), dtype=jnp.float32)}
        return inp
    _L0_gnn_all = _L0_gnn_setup()
    _L0_gnn_in = {k: v for k, v in _L0_gnn_all.items() if k in ('W1', 'b1', 'W2', 'b2', 'Wg', 'bg')}
    del _L0_gnn_all

    def _L1_gnn_setup():
        import jax, jax.numpy as jnp
        import numpy as np
        N_NODES = 3125
        N_EDGES = 50000
        IN_FEAT = 64
        OUT_FEAT = 64
        NUM_RELS = 32
        NUM_BASES = 8
        key = jax.random.key(seed)
        k = jax.random.split(key, 8)
        feat = jax.random.normal(k[0], (N_NODES, IN_FEAT), dtype=jnp.float32)
        coeff = jax.random.normal(k[1], (NUM_RELS, NUM_BASES), dtype=jnp.float32) * (1.0 / np.sqrt(NUM_RELS))
        W = jax.random.normal(k[2], (NUM_BASES, IN_FEAT, OUT_FEAT), dtype=jnp.float32) * (1.0 / np.sqrt(IN_FEAT))
        h_bias = jnp.zeros((OUT_FEAT,), dtype=jnp.float32)
        loop_weight = jax.random.normal(k[3], (IN_FEAT, OUT_FEAT), dtype=jnp.float32) * (1.0 / np.sqrt(IN_FEAT))
        src = jax.random.randint(k[4], (N_EDGES,), 0, N_NODES, dtype=jnp.int64)
        dst = jnp.sort(jax.random.randint(k[5], (N_EDGES,), 0, N_NODES, dtype=jnp.int64))
        etypes = jax.random.randint(k[6], (N_EDGES,), 0, NUM_RELS, dtype=jnp.int64)
        return {'feat': feat, 'coeff': coeff, 'W': W, 'h_bias': h_bias, 'loop_weight': loop_weight, 'src': src, 'dst': dst, 'etypes': etypes}
    _L1_gnn_all = _L1_gnn_setup()
    _L1_gnn_in = {k: v for k, v in _L1_gnn_all.items() if k in ('coeff', 'W', 'h_bias', 'loop_weight')}
    del _L1_gnn_all
    return {'x': x, 'src': src, 'dst': dst, 'edge_type_32': edge_type_32, 'L0_gnn_W1': _L0_gnn_in['W1'], 'L0_gnn_b1': _L0_gnn_in['b1'], 'L0_gnn_W2': _L0_gnn_in['W2'], 'L0_gnn_b2': _L0_gnn_in['b2'], 'L0_gnn_Wg': _L0_gnn_in['Wg'], 'L0_gnn_bg': _L0_gnn_in['bg'], 'L1_gnn_coeff': _L1_gnn_in['coeff'], 'L1_gnn_W': _L1_gnn_in['W'], 'L1_gnn_h_bias': _L1_gnn_in['h_bias'], 'L1_gnn_loop_weight': _L1_gnn_in['loop_weight']}

def reference(x, src, dst, edge_type_32, L0_gnn_W1, L0_gnn_b1, L0_gnn_W2, L0_gnn_b2, L0_gnn_Wg, L0_gnn_bg, L1_gnn_coeff, L1_gnn_W, L1_gnn_h_bias, L1_gnn_loop_weight):
    import jax
    import jax.numpy as jnp

    def _L0_gnn_ref(node_emb, edge_index, W1, b1, W2, b2, Wg, bg):
        import jax, jax.numpy as jnp
        import numpy as np
        src, dst = (edge_index[0], edge_index[1])
        pair_emb = jnp.concatenate([node_emb[src], node_emb[dst]], axis=-1)
        h = jax.nn.relu(pair_emb @ W1 + b1)
        interaction = h @ W2 + b2
        gate = jax.nn.sigmoid(interaction @ Wg + bg)
        gated = interaction * gate
        N = node_emb.shape[0]
        summed = jax.ops.segment_sum(gated, src, num_segments=N)
        counts = jax.ops.segment_sum(jnp.ones((src.shape[0],), dtype=gated.dtype), src, num_segments=N)
        pooled = summed / jnp.maximum(counts, 1.0)[:, None]
        return pooled

    def _L1_gnn_ref(feat, coeff, W, h_bias, loop_weight, src, dst, etypes):
        import jax, jax.numpy as jnp
        import numpy as np
        N_NODES = 3125
        N_EDGES = 50000
        IN_FEAT = 64
        OUT_FEAT = 64
        NUM_RELS = 32
        NUM_BASES = 8
        N, F = feat.shape
        R, B = coeff.shape
        O = W.shape[-1]
        seg = dst * R + etypes
        msgs = feat[src]
        agg_rel = jax.ops.segment_sum(msgs, seg, num_segments=N * R)
        agg_rel = agg_rel.reshape(N, R, F)
        agg = jnp.einsum('nrf,rb->nbf', agg_rel, coeff).reshape(N, B * F)
        h = agg @ W.reshape(B * F, O)
        h = h + h_bias
        h = h + feat @ loop_weight
        return jax.nn.relu(h)
    edge_index = jnp.stack([src, dst])
    h = jnp.maximum(_layernorm(x, axis=-1), 0.0)
    x = x + _L0_gnn_ref(h, edge_index, L0_gnn_W1, L0_gnn_b1, L0_gnn_W2, L0_gnn_b2, L0_gnn_Wg, L0_gnn_bg)
    h = jnp.maximum(_layernorm(x, axis=-1), 0.0)
    x = x + _L1_gnn_ref(h, L1_gnn_coeff, L1_gnn_W, L1_gnn_h_bias, L1_gnn_loop_weight, src, dst, edge_type_32)
    return x

_drawn_inputs = setup_inputs


def setup_inputs(seed=0):
    import zlib

    import numpy as np

    out = dict(_drawn_inputs(seed))
    spreads = {'L0_gnn_b1': (0.0, 0.285),
     'L0_gnn_b2': (0.0, 0.1),
     'L0_gnn_bg': (0.0, 0.8),
     'L1_gnn_h_bias': (0.0, 0.1)}
    factors = {}
    for name, (base, spread) in spreads.items():
        noise = np.random.default_rng([zlib.crc32(name.encode()), seed]).standard_normal(out[name].shape)
        drawn = base * np.exp(spread * noise) if base else spread * noise
        out[name] = jnp.asarray(drawn.astype(out[name].dtype))
    for name, factor in factors.items():
        out[name] = (out[name] * factor).astype(out[name].dtype)
    return out
```

```python
from contextlib import ExitStack

import concourse.bass as bass
from concourse import mybir

ALU = mybir.AluOpType
ACT = mybir.ActivationFunctionType
AX = mybir.AxisListType
F32 = mybir.dt.float32
F16 = mybir.dt.float16
BF16 = mybir.dt.bfloat16
I32 = mybir.dt.int32
ds = bass.ds

N = 50000
E = 50000
D = 64
RELS, BASES = 32, 8
P = 128
R = 4
GN = P * R
NG = -(-N // GN)
LASTP = (N - (NG - 1) * GN) // R
EP, ET = 125, 400
TG = 4
SG = ET // TG
NT = NG * TG
ES = NT // TG
STEPS = ES + NG - 1
W = D + 1
EPS = 1e-5
NB = NG // 2
BT = 2 * R
assert EP * ET == E and NT * P >= E and ES == NG and NB * 2 == NG and (N - (NG - 1) * GN) % R == 0


def gnn_kernel(nc, x, src, dst, etype, w1, b1, w2, b2, wg, bg, coeff, wb, hbias, loopw, out):
    with ExitStack() as ctx:
        def sb(name, shape, dt=F32):
            return ctx.enter_context(nc.sbuf_tensor(name, shape, dt))

        def ps(name, dt=F32, cols=512):
            return ctx.enter_context(nc.psum_tensor(name, [P, cols], dt))

        def sem(name):
            return ctx.enter_context(nc.semaphore(name))

        h_dram = nc.dram_tensor("h_rows", [N, D], F32)
        h1_dram = nc.dram_tensor("h1_rows", [N, D], F32)
        x1_dram = nc.dram_tensor("x1_rows", [N, D], F32)

        T = sb("node_table", [P, NG, R, W])
        iota512 = sb("iota512", [P, GN])
        iota16 = sb("iota16", [P, NT], F16)
        iota_i = sb("iota_i", [P, GN], I32)
        rel3 = sb("rel3", [P, 3 * RELS], F16)
        group_base = sb("group_base", [P, NG])
        ident = sb("ident", [P, P])
        ident16 = sb("ident16", [P, P], F16)
        tri = sb("tri", [P, P], F16)
        trc = sb("trc", [P, P], F16)
        ones16 = sb("ones16", [P, P], F16)
        ones32 = sb("ones32", [P, P])
        zero16 = sb("zero16", [P, 512], F16)
        eps = sb("eps", [P, 1])

        e_src = sb("e_src", [EP, ET], I32)
        e_dst = sb("e_dst", [EP, ET], I32)
        e_typ = sb("e_typ", [EP, ET], I32)
        e_tmp = sb("e_tmp", [EP, ET], I32)
        e_tm2 = sb("e_tm2", [EP, ET], I32)
        e_tm3 = sb("e_tm3", [EP, ET], I32)
        part = [sb(f"part{c}", [EP, ET]) for c in range(4)]
        key = [sb(f"key{s}", [EP, ET]) for s in range(2)]
        pos_f = sb("pos_f", [EP, ET])
        place_hi = sb("place_hi", [EP, ET])
        place_lo = sb("place_lo", [EP, ET])
        key_hot = [sb(f"key_hot{b}", [EP, TG, NG], F16) for b in range(2)]
        junk = sb("junk", [EP, TG, NG])
        rank4 = sb("rank4", [EP, TG])
        totals = sb("totals", [P, NG])
        starts = sb("starts", [P, NG])
        hi_hot = [sb(f"hi_hot{b}", [EP, NT], F16) for b in range(2)]
        lo_hot = [sb(f"lo_hot{b}", [EP, 4, P], F16) for b in range(2)]
        dec = [sb(f"dec{c}", [P, NT]) for c in range(3)]
        dec_i = [sb(f"dec_i{c}", [P, NT], I32) for c in range(2)]
        node = [sb(f"segment_node{s}", [P, NT]) for s in range(2)]
        srt_src = [sb(f"sorted_src{s}", [P, NT + 2 * TG], I32) for s in range(2)]
        srt_dst = sb("sorted_dst", [P, NT + 2 * TG], I32)
        srt_typ = sb("sorted_typ", [P, NT])
        first_group = [sb(f"first_group{s}", [1, ES + 1], I32) for s in range(2)]

        idx = [sb(f"idx{b}", [P, 2, TG], I32) for b in range(2)]
        rows = [sb(f"rows{b}", [P, TG, 2, D]) for b in range(2)]
        rowsT = sb("rowsT", [P, TG * P])
        hidT = sb("hidT", [D + 1, TG * P])
        gate = sb("gate", [P, TG, D])
        msg = sb("msg", [P, TG, W])
        hot = [sb(f"hot{b}", [P, R, P]) for b in range(2)]
        rel_hot = sb("rel_hot", [P, TG, 3 * RELS], F16)
        rel_hotT = sb("rel_hotT", [3 * RELS, TG * P], BF16)
        scaled = [sb(f"scaled{c}", [P, TG * P]) for c in range(4)]

        xb = [sb(f"xb{b}", [P, BT, D]) for b in range(2)]
        hb = [sb(f"hb{b}", [P, BT, D]) for b in range(2)]
        x1b = [sb(f"x1b{b}", [P, BT, D]) for b in range(2)]
        cen = sb("cen", [P, BT, D])
        sq = sb("sq", [P, BT, D])
        hbT = sb("hbT", [P, 512])
        st = sb("st", [P, 6, BT])

        w1s = sb("w1s", [2 * D, D])
        b1s = sb("b1s", [D, 1])
        w2s = sb("w2s", [D + 1, 2 * D])
        w2T = sb("w2T", [D, D + 1])
        wgs = sb("wgs", [D, D])
        bgs = sb("bgs", [D + 1, D])
        c3 = sb("c3", [3 * RELS, BASES])
        c3r = sb("c3r", [3 * RELS, BASES])
        c3b = [sb(f"c3b{k}", [3 * RELS, BASES], BF16) for k in range(3)]
        cpart = sb("cpart", [3 * RELS, BASES], BF16)
        crep = sb("crep", [3 * RELS, BASES, D], BF16)
        wbs = sb("wbs", [P, 4, D])
        loop2 = sb("loop2", [P, P])
        hbias_s = sb("hbias_s", [P, D])

        pk = [ps(f"pk{i}") for i in range(4)]
        p_run = ps("p_run")
        p_tr = ps("p_tr")
        p_mm = ps("p_mm")
        p_out = ps("p_out")
        p_tr16 = p_mm[:, :].bitcast(F16)
        step_sum = p_run[:, 0:R * W].rearrange("p (r w) -> p r w", w=W)

        consts = sem("consts")
        loaded_edges = sem("loaded_edges")
        loaded_w = sem("loaded_w")
        vdone = sem("vector_done")
        wprep = sem("weights_prepared")
        w2_turned = sem("w2_turned")
        w2_copied = sem("w2_copied")
        w2_folded = sem("w2_folded")
        weights_ready = sem("weights_ready")
        key_ready = [sem(f"key_hot_ready{b}") for b in range(2)]
        key_used = [sem(f"key_hot_used{b}") for b in range(2)]
        starts_ready = sem("starts_ready")
        ranks_ready = sem("ranks_ready")
        ranks_read = sem("ranks_read")
        place_ready = [sem(f"place_hot_ready{b}") for b in range(2)]
        place_used = [sem(f"place_hot_used{b}") for b in range(2)]
        pieces_read = sem("pieces_read")
        x_loaded = [sem(f"x_loaded{b}") for b in range(2)]
        centred = sem("centred")
        squared = sem("squared")
        var_ready = sem("var_ready")
        dev_ready = sem("dev_ready")
        hb_ready = [sem(f"hb_ready{b}") for b in range(2)]
        hb_stored = [sem(f"hb_stored{b}") for b in range(2)]
        h1_turned = sem("h1_turned")
        h1_copied = sem("h1_copied")
        looped = sem("looped")
        loop_added = sem("loop_added")
        sorted_ready = sem("sorted_ready")
        idx_ready = [sem(f"idx_ready{b}") for b in range(2)]
        gathered = [sem(f"gathered{b}") for b in range(2)]
        gathers_started = sem("gathers_started")
        doubled = sem("rows_doubled")
        rows_turned = sem("rows_turned")
        turned_copied = sem("turned_copied")
        hid_ready = sem("hid_ready")
        hidT_ready = sem("hidT_ready")
        pre_ready = sem("pre_ready")
        gate_ready = sem("gate_ready")
        msg_ready = sem("msg_ready")
        rel_ready = sem("rel_ready")
        rel_turned = sem("rel_turned")
        relT_ready = sem("relT_ready")
        cof_ready = sem("cof_ready")
        scaled_ready = sem("scaled_ready")
        edge_out = sem("edge_out")
        hot_ready = [sem(f"hot_ready{b}") for b in range(2)]
        hot_used = [sem(f"hot_used{b}") for b in range(2)]
        step_added = sem("step_added")
        out_ready = [sem(f"out_ready{b}") for b in range(2)]
        out_stored = [sem(f"out_stored{b}") for b in range(2)]

        block = ctx.enter_context(nc.Block())

        def blocks(ap):
            full = ap[0:(NG - 2) * GN, :].rearrange("(g p r) f -> g p (r f)", p=P, r=R)
            return full

        def block_dma(eng, dram, tile, q, load, signal):
            t = tile[:, :, :].rearrange("p (g r) f -> p g (r f)", g=2)
            if q is not None:
                d = blocks(dram)[ds(q * 2, 2)].rearrange("g p x -> p g x")
                pairs = [(d, t)]
            else:
                lo = (NG - 2) * GN
                d0 = dram[lo:lo + GN, :].rearrange("(p r) f -> p (r f)", r=R)
                d1 = dram[lo + GN:N, :].rearrange("(p r) f -> p (r f)", r=R)
                pairs = [(d0, t[:, 0, :]), (d1, t[0:LASTP, 1, :])]
            for d, s in pairs:
                a, b = (s, d) if load else (d, s)
                eng.dma_start(a, b).then_inc(signal, 16)

        PAIRS = (NB - 1) // 2
        assert PAIRS * 2 + 1 == NB

        def over_blocks(eng, body):
            with eng.Fori(0, PAIRS) as i:
                for b in range(2):
                    body(i * 2 + b, b, i)
            body(None, 0, PAIRS)

        def moved(q, uses):
            return (uses + 1) * 16 if q is not None else uses * 16 + 32

        def moved_pass(b):
            return PAIRS * 16 + (0 if b else 32)

        own = [0, 0, 0]

        def done(ins):
            ins.then_inc(vdone, 1)
            own[1] += 1
            nc.vector.wait_ge(vdone, own[0] + own[1])

        def loop_starts():
            own[2] = own[0] + own[1]

        def turn(i, per):
            own[0], own[1] = own[2] + i * per, 0

        def loop_ends(turns, per):
            assert own[1] == per, (own[1], per)
            own[0], own[1] = own[2] + turns * per, 0

        @block.sync
        def _(sp):
            for t, a in ((e_src, src), (e_dst, dst), (e_typ, etype)):
                sp.dma_start(t[:, :], a.rearrange("(p t) -> p t", p=EP)).then_inc(loaded_edges, 16)
            n = 0
            for t, a in ((w1s[:, :], w1), (b1s[:, :], b1.rearrange("(p o) -> p o", o=1)),
                         (w2s[0:D, 0:D], w2), (w2s[D:D + 1, 0:D], b2.rearrange("(o f) -> o f", o=1)),
                         (wgs[:, :], wg),
                         (c3[0:RELS, :], coeff), (c3[RELS:2 * RELS, :], coeff), (c3[2 * RELS:3 * RELS, :], coeff),
                         (wbs[:, :, :], wb.rearrange("b f o -> (b f) o").rearrange("(c p) o -> p c o", p=P)),
                         (hbias_s[:, :], hbias.rearrange("(o f) -> o f", o=1).broadcast_to([P, D]))):
                sp.dma_start(t, a).then_inc(loaded_w, 16)
                n += 16
            sp.wait_ge(wprep, 3)
            sp.dma_start(loop2[0:D, 0:D], loopw).then_inc(loaded_w, 16)
            sp.dma_start(loop2[D:P, D:P], loopw).then_inc(loaded_w, 16)
            sp.dma_start(bgs[D:D + 1, :], bg.rearrange("(o f) -> o f", o=1)).then_inc(loaded_w, 16)

            def load(dram, read, before):
                def body(q, b, uses):
                    sp.wait_ge(read[b], before * (PAIRS + 1 - b) + uses)
                    block_dma(sp, dram, xb[b], q, True, x_loaded[b])
                over_blocks(sp, body)

            load(x, hb_ready, 0)
            load(x, hb_ready, 1)
            for b in range(2):
                sp.wait_ge(hb_ready[b], 2 * (PAIRS + 1 - b))
                sp.wait_ge(hb_stored[b], 3 * moved_pass(b))
            load(x1_dram, out_ready, 0)

        @block.gpsimd
        def _(pool):
            pool.memset(iota_i[:, 0:1], 0).then_inc(consts, 1)
            nc.gpsimd.iota(iota512[:, :], [[1, R], [R, P]], base=0, channel_multiplier=0,
                           allow_small_or_imprecise_dtypes=True).then_inc(consts, 1)
            nc.gpsimd.iota(iota16[:, :], [[1, NT]], base=0, channel_multiplier=0,
                           allow_small_or_imprecise_dtypes=True).then_inc(consts, 1)
            nc.gpsimd.iota(rel3[:, :], [[0, 3], [1, RELS]], base=0, channel_multiplier=0,
                           allow_small_or_imprecise_dtypes=True).then_inc(consts, 1)
            nc.gpsimd.iota(group_base[:, :], [[GN, NG]], base=0, channel_multiplier=0,
                           allow_small_or_imprecise_dtypes=True).then_inc(consts, 1)
            nc.gpsimd.iota(ones32[:, :], [[1, P]], base=0, channel_multiplier=-1,
                           allow_small_or_imprecise_dtypes=True).then_inc(consts, 1)

            def store_h(q, b, uses):
                pool.wait_ge(hb_ready[b], uses + 1)
                block_dma(pool, h_dram, hb[b], q, False, hb_stored[b])
            over_blocks(pool, store_h)

            def gathers(layer, base, used, used_before):
                table = h_dram if layer == 0 else h1_dram
                per = 2 if layer == 0 else 1
                with pool.Fori(0, ES // 2) as i:
                    for b in range(2):
                        pool.wait_ge(idx_ready[b], base + i + 1)
                        pool.wait_ge(used, used_before + i * 2 + b)
                        pool.sem_inc(gathers_started, 1)
                        for u in range(TG):
                            for e in range(per):
                                pool.indirect_dma_start(
                                    out=rows[b][:, u, e, :], out_offset=None, in_=table[:, :],
                                    in_offset=bass.IndirectOffsetOnAxis(ap=idx[b][:, e, u:u + 1], axis=0)).then_inc(gathered[b], 16)

            for b in range(2):
                pool.wait_ge(hb_stored[b], moved_pass(b))
            pool.sem_inc(rows_turned, 1)
            gathers(0, 0, rows_turned, 0)

            def store_x1h1(q, b, uses):
                pool.wait_ge(hb_ready[b], (PAIRS + 1 - b) + uses + 1)
                block_dma(pool, x1_dram, x1b[b], q, False, hb_stored[b])
                block_dma(pool, h1_dram, hb[b], q, False, hb_stored[b])
            over_blocks(pool, store_x1h1)
            for b in range(2):
                pool.wait_ge(hb_stored[b], 3 * moved_pass(b))
            pool.wait_ge(rows_turned, ES + 1)
            gathers(1, ES // 2 + 1, rows_turned, ES)

            def store_out(q, b, uses):
                pool.wait_ge(out_ready[b], uses + 1)
                block_dma(pool, out, hb[b], q, False, out_stored[b])
            over_blocks(pool, store_out)
            for b in range(2):
                pool.wait_ge(out_stored[b], moved_pass(b))

        @block.scalar
        def _(act):
            act.wait_ge(w2_turned, 1)
            nc.scalar.activation(w2T[:, :], p_tr[0:D, 0:D + 1], ACT.Copy).then_inc(w2_copied, 1)

            act.wait_ge(wprep, 3)
            def norm(base):
                def body(q, b, uses):
                    c = base + (uses * 2 + b if q is not None else NB - 1)
                    act.wait_ge(centred, c + 1)
                    nc.scalar.activation(sq[:, :, :], cen[:, :, :], ACT.Square).then_inc(squared, 1)
                    act.wait_ge(var_ready, c + 1)
                    nc.scalar.activation(st[:, 3, :], st[:, 2, :], ACT.Sqrt, bias=eps[:, 0:1],
                                         scale=1.0 / D).then_inc(dev_ready, 1)
                    if base:
                        act.wait_ge(h1_turned, c - NB + 1)
                        nc.scalar.activation(hbT[:, :], p_tr[:, :], ACT.Copy).then_inc(h1_copied, 1)
                return body
            over_blocks(act, norm(0))

            with act.Fori(0, ES) as s:
                act.wait_ge(rows_turned, s + 2)
                nc.scalar.activation(rowsT[:, :], p_tr[:, :], ACT.Copy).then_inc(turned_copied, 1)
                act.wait_ge(hid_ready, s + 1)
                nc.scalar.activation(hidT[0:D, :], p_mm[0:D, :], ACT.Relu, bias=b1s[:, 0:1]).then_inc(hidT_ready, 1)
                act.wait_ge(pre_ready, s + 1)
                nc.scalar.activation(gate[:, :, :], p_out[:, :].rearrange("p (u e f) -> p u e f", u=TG, e=2)[:, :, 1, :],
                                     ACT.Tanh, scale=0.5).then_inc(gate_ready, 1)
                act.wait_ge(msg_ready, s + 1)

            over_blocks(act, norm(NB))

            with act.Fori(0, ES // 2) as i:
                for b in range(2):
                    s = i * 2 + b
                    act.wait_ge(gathered[b], 16 * TG * (2 * (ES // 2) + i + 1))
                    nc.scalar.activation(rows[b][:, :, 1, :], rows[b][:, :, 0, :], ACT.Copy).then_inc(doubled, 1)
                    act.wait_ge(rel_turned, s + 1)
                    nc.scalar.activation(rel_hotT[:, :], p_tr16[0:3 * RELS, 0:TG * P], ACT.Copy).then_inc(relT_ready, 1)
                    act.wait_ge(rows_turned, ES + s + 2)
                    nc.scalar.activation(rowsT[:, :], p_tr[:, :], ACT.Copy).then_inc(turned_copied, 1)
                    act.wait_ge(edge_out, s + 1)
                    nc.scalar.activation(msg[:, :, 0:D],
                                         p_out[:, 0:TG * D].rearrange("p (u f) -> p u f", u=TG),
                                         ACT.Copy).then_inc(msg_ready, 1)

        @block.tensor
        def _(pe):
            mm = nc.tensor.matmul
            pe.wait_ge(loaded_w, 13 * 16)
            pe.wait_ge(wprep, 3)
            nc.tensor.transpose(p_tr[0:D, 0:D + 1], w2s[:, 0:D], ident[0:D + 1, 0:D + 1]).then_inc(w2_turned, 1)
            pe.wait_ge(w2_copied, 1)
            mm(p_mm[0:D + 1, 0:D], w2T[:, :], wgs[:, :], start=True, stop=True).then_inc(w2_folded, 1)

            def zero(bank, cols):
                return mm(bank[:, 0:cols], zero16[0:EP, 0:P], zero16[0:EP, 0:cols], start=True, stop=False,
                          skip_group_check=True)

            def add(out_, lhsT, rhs):
                return mm(out_, lhsT, rhs, start=False, stop=False, skip_group_check=True)

            def sort(s):
                zero(p_run, NG)
                with pe.Fori(0, SG // 2) as i:
                    for b in range(2):
                        pe.wait_ge(key_ready[b], 2 * s * (SG // 2) + i + 1)
                        for u in range(TG):
                            m = add(p_run[:, 0:NG], ones16[0:EP, :], key_hot[b][:, u, :])
                        m.then_inc(key_used[b], 1)
                pe.wait_ge(starts_ready, s + 1)
                for u in range(TG):
                    mm(p_run[:, u * NG:(u + 1) * NG], ones32[0:1, :], starts[0:1, :], start=(u == 0), stop=False,
                       skip_group_check=True)

                def slot(u):
                    return p_run[:, u * NG:(u + 1) * NG]

                with pe.Fori(0, SG // 2) as i:
                    for b in range(2):
                        pe.wait_ge(key_ready[b], (2 * s + 1) * (SG // 2) + i + 1)
                        m = add(p_run[:, 0:TG * NG], tri[0:EP, :], key_hot[b][:, :, :].rearrange("p u g -> p (u g)"))
                        for u in range(TG):
                            for v in range(u):
                                m = add(slot(u), ones16[0:EP, :], key_hot[b][:, v, :])
                        m.then_inc(ranks_ready, 1)
                        pe.wait_ge(ranks_read, s * SG + i * 2 + b + 1)
                        m = add(p_run[:, 0:TG * NG], trc[0:EP, :], key_hot[b][:, :, :].rearrange("p u g -> p (u g)"))
                        for u in range(TG):
                            for v in range(u + 1, TG):
                                m = add(slot(u), ones16[0:EP, :], key_hot[b][:, v, :])
                        m.then_inc(key_used[b], 1)
                if s:
                    pe.wait_ge(pieces_read, s)
                for c in range(3 + s):
                    zero(pk[c], NT)
                with pe.Fori(0, ET // 2) as i:
                    for b in range(2):
                        pe.wait_ge(place_ready[b], s * (ET // 2) + i + 1)
                        for c in range(3 + s):
                            m = add(pk[c][:, 0:NT], lo_hot[b][:, c, :], hi_hot[b][:, :])
                        m.then_inc(place_used[b], 1)

            sort(0)
            sort(1)
            pe.wait_ge(sorted_ready, 1)

            def steps(layer, s):
                g0 = pe.value_load(first_group[layer][0:1, ds(s, 1)], min_val=0, max_val=NG - 1)
                g1 = pe.value_load(first_group[layer][0:1, ds(s + 1, 1)], min_val=0, max_val=NG - 1)
                with pe.Fori(g0, g1 + 1) as g:
                    pe.wait_ge(msg_ready, layer * ES + s + 1)
                    k = s + g + layer * STEPS
                    pe.wait_ge(step_added, k)
                    for u in range(TG):
                        pe.wait_ge(hot_ready[u % 2], k * 2 + u // 2 + 1)
                        for r in range(R):
                            m = mm(step_sum[:, r, :], hot[u % 2][:, r, :], msg[:, u, :],
                                   start=(u == 0 and r == 0), stop=(u == TG - 1 and r == R - 1),
                                   skip_group_check=True)
                        m.then_inc(hot_used[u % 2], 1)

            pe.wait_ge(weights_ready, 1)
            with pe.Fori(0, ES // 2) as i:
                for b in range(2):
                    s = i * 2 + b
                    pe.wait_ge(gathered[b], 2 * 16 * TG * (i + 1))
                    pe.wait_ge(turned_copied, s)
                    for u in range(TG):
                        m = nc.tensor.transpose(p_tr[:, u * P:(u + 1) * P],
                                                rows[b][:, u, :, :].rearrange("p e f -> p (e f)"), ident[:, :])
                    m.then_inc(rows_turned, 1)
                    pe.wait_ge(turned_copied, s + 1)
                    mm(p_mm[0:D, :], w1s[:, :], rowsT[:, :], start=True, stop=True).then_inc(hid_ready, 1)
                    pe.wait_ge(hidT_ready, s + 1)
                    pe.wait_ge(msg_ready, s)
                    for u in range(TG):
                        m = mm(p_out[:, u * P:(u + 1) * P], hidT[:, u * P:(u + 1) * P], w2s[:, :],
                               start=(u == 0), stop=(u == TG - 1), skip_group_check=True)
                    m.then_inc(pre_ready, 1)
                    steps(0, s)

            def loop_block(q, b, uses):
                c = uses * 2 + b if q is not None else NB - 1
                pe.wait_ge(hb_ready[b], (PAIRS + 1 - b) + uses + 1)
                pe.wait_ge(h1_copied, c)
                for j in range(4):
                    m = nc.tensor.transpose(p_tr[:, j * P:(j + 1) * P],
                                            hb[b][:, 2 * j:2 * j + 2, :].rearrange("p t f -> p (t f)"), ident[:, :])
                m.then_inc(h1_turned, 1)
                pe.wait_ge(h1_copied, c + 1)
                pe.wait_ge(loop_added, c)
                for j in range(4):
                    m = mm(p_out[:, j * P:(j + 1) * P], hbT[:, j * P:(j + 1) * P], loop2[:, :],
                           start=(j == 0), stop=(j == 3), skip_group_check=True)
                m.then_inc(looped, 1)
            over_blocks(pe, loop_block)

            with pe.Fori(0, ES // 2) as i:
                for b in range(2):
                    s = i * 2 + b
                    pe.wait_ge(rel_ready, s + 1)
                    pe.wait_ge(relT_ready, s)
                    for u in range(TG):
                        m = nc.tensor.transpose(p_tr16[0:3 * RELS, u * P:(u + 1) * P], rel_hot[:, u, :], ident16[:, :])
                    m.then_inc(rel_turned, 1)
                    pe.wait_ge(doubled, s + 1)
                    pe.wait_ge(turned_copied, ES + s)
                    for u in range(TG):
                        m = nc.tensor.transpose(p_tr[:, u * P:(u + 1) * P],
                                                rows[b][:, u, :, :].rearrange("p e f -> p (e f)"), ident[:, :])
                    m.then_inc(rows_turned, 1)
                    pe.wait_ge(relT_ready, s + 1)
                    pe.wait_ge(scaled_ready, 4 * s)
                    for c in range(4):
                        mm(pk[c][:, :], crep[:, 2 * c:2 * c + 2, :].rearrange("p b f -> p (b f)"), rel_hotT[:, :],
                           start=True, stop=True).then_inc(cof_ready, 1)
                    pe.wait_ge(scaled_ready, 4 * s + 4)
                    pe.wait_ge(msg_ready, ES + s)
                    for u in range(TG):
                        for c in range(4):
                            m = mm(p_out[:, u * D:(u + 1) * D], scaled[c][:, u * P:(u + 1) * P], wbs[:, c, :],
                                   start=(u == 0 and c == 0), stop=(u == TG - 1 and c == 3), skip_group_check=True)
                    m.then_inc(edge_out, 1)
                    steps(1, s)

        @block.vector
        def _(dve):
            v = nc.vector
            dve.wait_ge(consts, 6)
            v.tensor_scalar(tri[:, :], ones32[:, :], 0.0, None, ALU.is_gt).then_inc(vdone, 1)
            v.tensor_scalar(trc[:, :], ones32[:, :], 0.0, None, ALU.is_le).then_inc(vdone, 1)
            v.tensor_scalar(ident[:, :], ones32[:, :], 0.0, None, ALU.is_equal).then_inc(vdone, 1)
            v.tensor_scalar(ident16[:, :], ones32[:, :], 0.0, None, ALU.is_equal).then_inc(vdone, 1)
            dve.wait_ge(vdone, 4)
            own[1] = 4
            done(v.memset(ones32[:, :], 1.0))
            v.memset(ones16[:, :], 1.0)
            v.memset(zero16[:, :], 0.0)
            v.memset(T[:, :, :, :], 0.0)
            v.memset(hidT[D:D + 1, :], 1.0)
            v.memset(msg[:, :, D:W], 1.0)
            for b in range(2):
                v.memset(xb[b][:, :, :], 0.0)
            for t in (srt_src[0], srt_src[1], srt_dst):
                v.memset(t[:, NT:NT + 2 * TG], 0)
            v.memset(loop2[:, :], 0.0).then_inc(wprep, 1)
            v.memset(bgs[:, :], 0.0).then_inc(wprep, 1)
            v.memset(eps[:, :], EPS).then_inc(wprep, 1)

            dve.wait_ge(loaded_w, 13 * 16)
            dve.wait_ge(w2_folded, 1)
            v.tensor_scalar(w2s[:, 0:D], w2s[:, 0:D], 0.5, None, ALU.mult)
            v.tensor_tensor(w2s[:, D:2 * D], p_mm[0:D + 1, 0:D], bgs[:, :], ALU.add).then_inc(weights_ready, 1)
            done(v.tensor_copy(c3b[0][:, :], c3[:, :]))
            done(v.tensor_tensor(c3r[:, :], c3[:, :], c3b[0][:, :], ALU.subtract))
            done(v.tensor_copy(c3b[1][:, :], c3r[:, :]))
            done(v.tensor_tensor(c3[:, :], c3r[:, :], c3b[1][:, :], ALU.subtract))
            done(v.tensor_copy(c3b[2][:, :], c3[:, :]))
            for k in range(3):
                done(v.tensor_copy(cpart[k * RELS:(k + 1) * RELS, :], c3b[k][k * RELS:(k + 1) * RELS, :]))
            done(v.tensor_copy(crep[:, :, :], cpart[:, :].rearrange("p (b o) -> p b o", o=1).broadcast_to([3 * RELS, BASES, D])))

            dve.wait_ge(loaded_edges, 48)
            done(v.tensor_scalar(e_tmp[:, :], e_src[:, :], 5, None, ALU.arith_shift_right))
            done(v.tensor_copy(part[0][:, :], e_tmp[:, :]))
            done(v.tensor_scalar(e_tmp[:, :], e_src[:, :], 31, 5, ALU.bitwise_and, ALU.logical_shift_left))
            done(v.tensor_scalar(e_tm2[:, :], e_dst[:, :], 11, None, ALU.arith_shift_right))
            done(v.tensor_tensor(e_tm3[:, :], e_tmp[:, :], e_tm2[:, :], ALU.bitwise_or))
            done(v.tensor_copy(part[1][:, :], e_tm3[:, :]))
            done(v.tensor_scalar(e_tmp[:, :], e_dst[:, :], 2047, None, ALU.bitwise_and))
            done(v.tensor_scalar(part[2][:, :], e_tmp[:, :], 1.0, None, ALU.add))
            done(v.tensor_copy(part[3][:, :], e_typ[:, :]))
            for k, e in enumerate((e_src, e_dst)):
                done(v.tensor_scalar(e_tmp[:, :], e[:, :], 9, None, ALU.arith_shift_right))
                done(v.tensor_copy(key[k][:, :], e_tmp[:, :]))

            def norm(X, H, c):
                done(v.tensor_reduce(st[:, 0, :], X, AX.X, ALU.add))
                done(v.tensor_scalar(st[:, 1, :], st[:, 0, :], 1.0 / D, None, ALU.mult))
                v.tensor_tensor(cen[:, :, :], X, st[:, 1, :].rearrange("p (t o) -> p t o", o=1).broadcast_to([P, BT, D]),
                                ALU.subtract).then_inc(centred, 1)
                dve.wait_ge(squared, c + 1)
                v.tensor_reduce(st[:, 2, :], sq[:, :, :], AX.X, ALU.add).then_inc(var_ready, 1)
                dve.wait_ge(dev_ready, c + 1)
                done(v.reciprocal(st[:, 4, :], st[:, 3, :]))
                return v.scalar_tensor_tensor(
                    out=H, in0=cen[:, :, :], scalar=0.0,
                    in1=st[:, 4, :].rearrange("p (t o) -> p t o", o=1).broadcast_to([P, BT, D]),
                    op0=ALU.max, op1=ALU.mult)

            def chained(body, per):
                loop_starts()
                with dve.Fori(0, PAIRS) as i:
                    for b in range(2):
                        turn(i * 2 + b, per)
                        body(i * 2 + b, b, i)
                loop_ends(2 * PAIRS, per)
                body(None, 0, PAIRS)

            def first(q, b, uses):
                c = uses * 2 + b if q is not None else NB - 1
                dve.wait_ge(x_loaded[b], moved(q, uses))
                dve.wait_ge(hb_stored[b], uses * 16)
                norm(xb[b][:, :, :], hb[b][:, :, :], c).then_inc(hb_ready[b], 1)
            chained(first, 3)

            def sort(s):
                def hots(b, i, base):
                    dve.wait_ge(key_used[b], base + i)
                    for u in range(TG):
                        t = i * (2 * TG) + b * TG + u
                        m = v.tensor_scalar(key_hot[b][:, u, :], iota16[0:EP, 0:NG], key[s][:, ds(t, 1)], None,
                                            ALU.is_equal)
                    m.then_inc(key_ready[b], 1)

                with dve.Fori(0, SG // 2) as i:
                    for b in range(2):
                        hots(b, i, 2 * s * (SG // 2))
                for b in range(2):
                    dve.wait_ge(key_used[b], (2 * s + 1) * (SG // 2))
                done(v.tensor_copy(totals[:, :], p_run[:, 0:NG]))
                done(v.tensor_tensor_scan(starts[:, :], ones32[:, 0:NG], totals[:, :], 0.0, ALU.mult, ALU.add))

                v.tensor_tensor(starts[:, :], starts[:, :], totals[:, :], ALU.subtract).then_inc(starts_ready, 1)
                dve.wait_ge(starts_ready, s + 1)
                loop_starts()
                with dve.Fori(0, SG // 2) as i:
                    for b in range(2):
                        turn(i * 2 + b, 1)
                        hots(b, i, (2 * s + 1) * (SG // 2))
                        dve.wait_ge(key_ready[b], (2 * s + 1) * (SG // 2) + i + 1)
                        dve.wait_ge(ranks_ready, s * SG + i * 2 + b + 1)
                        for u in range(TG):
                            m = v.tensor_tensor_reduce(junk[:, u, :], p_run[0:EP, u * NG:(u + 1) * NG], key_hot[b][:, u, :],
                                                       1.0, 0.0, ALU.mult, ALU.add, rank4[:, u:u + 1])
                        m.then_inc(ranks_read, 1)
                        dve.wait_ge(ranks_read, s * SG + i * 2 + b + 1)
                        done(v.tensor_copy(pos_f[:, ds(i * (2 * TG) + b * TG, TG)], rank4[:, :]))
                loop_ends(SG, 1)
                done(v.tensor_copy(e_tmp[:, :], pos_f[:, :]))
                done(v.tensor_scalar(e_tm2[:, :], e_tmp[:, :], 7, None, ALU.arith_shift_right))
                done(v.tensor_scalar(e_tm3[:, :], e_tmp[:, :], P - 1, None, ALU.bitwise_and))
                done(v.tensor_copy(place_hi[:, :], e_tm2[:, :]))
                done(v.tensor_copy(place_lo[:, :], e_tm3[:, :]))
                with dve.Fori(0, ET // 2) as i:
                    for b in range(2):
                        dve.wait_ge(place_used[b], s * (ET // 2) + i)
                        t = i * 2 + b
                        v.tensor_scalar(hi_hot[b][:, :], iota16[0:EP, :], place_hi[:, ds(t, 1)], None, ALU.is_equal)
                        for c in range(3 + s):
                            m = v.tensor_scalar(lo_hot[b][:, c, :], iota16[0:EP, 0:P], place_lo[:, ds(t, 1)],
                                                part[c][:, ds(t, 1)], ALU.is_equal, ALU.mult)
                        m.then_inc(place_ready[b], 1)
                for b in range(2):
                    dve.wait_ge(place_used[b], (s + 1) * (ET // 2))
                done(v.tensor_copy(dec_i[0][:, :], pk[1][:, 0:NT]))
                done(v.tensor_scalar(dec_i[1][:, :], dec_i[0][:, :], 5, None, ALU.arith_shift_right))
                done(v.tensor_copy(dec[0][:, :], dec_i[1][:, :]))
                done(v.scalar_tensor_tensor(out=dec[1][:, :], in0=pk[0][:, 0:NT], scalar=32.0, in1=dec[0][:, :],
                                            op0=ALU.mult, op1=ALU.add))
                done(v.tensor_copy(srt_src[s][:, 0:NT], dec[1][:, :]))
                done(v.tensor_scalar(dec_i[1][:, :], dec_i[0][:, :], 31, None, ALU.bitwise_and))
                done(v.tensor_copy(dec[0][:, :], dec_i[1][:, :]))
                done(v.tensor_scalar(dec[2][:, :], pk[2][:, 0:NT], -1.0, 0.0, ALU.add, ALU.max))
                done(v.scalar_tensor_tensor(out=dec[2][:, :], in0=dec[0][:, :], scalar=2048.0, in1=dec[2][:, :],
                                            op0=ALU.mult, op1=ALU.add))
                if s == 0:
                    done(v.tensor_copy(srt_dst[:, 0:NT], dec[2][:, :]))
                else:
                    done(v.tensor_copy(srt_typ[:, :], pk[3][:, 0:NT]))
                seg = dec[1] if s == 0 else dec[2]
                done(v.tensor_copy(dec_i[0][0:1, :], seg[0:1, :]))
                done(v.tensor_scalar(dec_i[1][0:1, :], dec_i[0][0:1, :], 9, None, ALU.arith_shift_right))
                done(v.tensor_copy(first_group[s][0:1, 0:ES],
                                   dec_i[1][0:1, :].rearrange("p (s u) -> p s u", u=TG)[:, :, 0]))
                done(v.memset(first_group[s][0:1, 0:1], 0))
                done(v.memset(first_group[s][0:1, ES:ES + 1], NG - 1))
                done(v.tensor_scalar(dec[0][:, :], pk[2][:, 0:NT], 0.0, -65536.0, ALU.is_equal, ALU.mult))
                v.tensor_tensor(node[s][:, :], seg[:, :], dec[0][:, :], ALU.add).then_inc(pieces_read, 1)
                dve.wait_ge(pieces_read, s + 1)

            sort(0)
            sort(1)
            v.memset(junk[:, 0, 0:1], 0.0).then_inc(sorted_ready, 1)

            def steps(layer, s):
                g0 = dve.value_load(first_group[layer][0:1, ds(s, 1)], min_val=0, max_val=NG - 1)
                g1 = dve.value_load(first_group[layer][0:1, ds(s + 1, 1)], min_val=0, max_val=NG - 1)
                with dve.Fori(g0, g1 + 1) as g:
                    k = s + g + layer * STEPS
                    for u in range(TG):
                        dve.wait_ge(hot_used[u % 2], k * 2 + u // 2)
                        v.tensor_scalar(hot[u % 2][:, :, :].rearrange("p r n -> p (r n)"), iota512[:, :],
                                        group_base[:, ds(g, 1)], node[layer][:, ds(s * TG + u, 1)],
                                        ALU.add, ALU.is_equal).then_inc(hot_ready[u % 2], 1)
                    dve.wait_ge(hot_used[1], k * 2 + 2)
                    dve.wait_ge(step_added, k)
                    tg = T[:, ds(g, 1), :, :].rearrange("p g r w -> p (g r w)")
                    v.tensor_tensor(tg, tg, p_run[:, 0:R * W], ALU.add).then_inc(step_added, 1)

            def put_idx(layer, b, i):
                at = ds(i * (2 * TG) + b * TG, TG)
                m = v.tensor_copy(idx[b][:, 0, :], srt_src[layer][:, at])
                if layer == 0:
                    m = v.tensor_copy(idx[b][:, 1, :], srt_dst[:, at])
                m.then_inc(idx_ready[b], 1)

            for b in range(2):
                put_idx(0, b, 0)
            with dve.Fori(0, ES // 2) as i:
                for b in range(2):
                    s = i * 2 + b
                    dve.wait_ge(gate_ready, s + 1)
                    v.scalar_tensor_tensor(out=msg[:, :, 0:D], in0=gate[:, :, :], scalar=1.0,
                                           in1=p_out[:, :].rearrange("p (u e f) -> p u e f", u=TG, e=2)[:, :, 0, :],
                                           op0=ALU.add, op1=ALU.mult).then_inc(msg_ready, 1)
                    dve.wait_ge(gathered[b], 2 * 16 * TG * (i + 1))
                    put_idx(0, b, i + 1)
                    steps(0, s)

            def second(q, b, uses):
                c = uses * 2 + b if q is not None else NB - 1
                Tb = (T[:, ds(q * 2, 2), :, :] if q is not None else T[:, NG - 2:NG, :, :]).rearrange("p g r w -> p (g r) w")
                dve.wait_ge(x_loaded[b], moved(q, uses) + moved_pass(b))
                dve.wait_ge(hb_stored[b], uses * 32 + moved_pass(b))
                done(v.tensor_scalar(st[:, 0, :], Tb[:, :, D:W].rearrange("p t w -> p (t w)"), 1.0, None, ALU.max))
                done(v.reciprocal(st[:, 1, :], st[:, 0, :]))
                done(v.tensor_tensor(cen[:, :, :], Tb[:, :, 0:D],
                                     st[:, 1, :].rearrange("p (t o) -> p t o", o=1).broadcast_to([P, BT, D]), ALU.mult))
                done(v.tensor_tensor(x1b[b][:, :, :], xb[b][:, :, :], cen[:, :, :], ALU.add))
                norm(x1b[b][:, :, :], hb[b][:, :, :], NB + c).then_inc(hb_ready[b], 1)
                dve.wait_ge(looped, c + 1)
                v.tensor_tensor(Tb[:, :, 0:D], p_out[:, :].rearrange("p (t f) -> p t f", f=D),
                                hbias_s[:, :].rearrange("p (o f) -> p o f", o=1).broadcast_to([P, BT, D]),
                                ALU.add).then_inc(loop_added, 1)
            dve.wait_ge(step_added, STEPS)
            chained(second, 7)
            dve.wait_ge(loop_added, NB)

            for b in range(2):
                dve.wait_ge(gathered[b], 2 * 16 * TG * (ES // 2))
            for b in range(2):
                put_idx(1, b, 0)
            with dve.Fori(0, ES // 2) as i:
                for b in range(2):
                    s = i * 2 + b
                    dve.wait_ge(rel_turned, s)
                    for u in range(TG):
                        m = v.tensor_scalar(rel_hot[:, u, :], rel3[:, :], srt_typ[:, ds(s * TG + u, 1)], None,
                                            ALU.is_equal)
                    m.then_inc(rel_ready, 1)
                    dve.wait_ge(gathered[b], 16 * TG * (2 * (ES // 2) + i + 1))
                    put_idx(1, b, i + 1)
                    dve.wait_ge(turned_copied, ES + s + 1)
                    dve.wait_ge(edge_out, s)
                    for c in range(4):
                        dve.wait_ge(cof_ready, 4 * s + c + 1)
                        v.tensor_tensor(scaled[c][:, :], pk[c][:, :], rowsT[:, :], ALU.mult).then_inc(scaled_ready, 1)
                    steps(1, s)
            dve.wait_ge(step_added, 2 * STEPS)

            def third(q, b, uses):
                Tb = (T[:, ds(q * 2, 2), :, :] if q is not None else T[:, NG - 2:NG, :, :]).rearrange("p g r w -> p (g r) w")
                dve.wait_ge(x_loaded[b], moved(q, uses) + 2 * moved_pass(b))
                dve.wait_ge(out_stored[b], uses * 16)
                v.scalar_tensor_tensor(out=hb[b][:, :, :], in0=Tb[:, :, 0:D], scalar=0.0, in1=xb[b][:, :, :],
                                       op0=ALU.max, op1=ALU.add).then_inc(out_ready[b], 1)
            over_blocks(dve, third)


_INS = ['x', 'src', 'dst', 'edge_type_32', 'L0_gnn_W1', 'L0_gnn_b1', 'L0_gnn_W2', 'L0_gnn_b2', 'L0_gnn_Wg', 'L0_gnn_bg',
        'L1_gnn_coeff', 'L1_gnn_W', 'L1_gnn_h_bias', 'L1_gnn_loop_weight']


def kernel(**inputs):
    import numpy as _np
    import concourse.bacc as _bacc
    from concourse import mybir as _mybir
    from concourse.bass_utils import run_bass_kernel_spmd as _run

    nc = _bacc.Bacc("TRN2", target_bir_lowering=False, num_devices=1)
    arrays, args = {}, []
    for name in _INS:
        a = _np.ascontiguousarray(inputs[name])
        arrays[f"in_{name}"] = a
        args.append(nc.dram_tensor(f"in_{name}", a.shape, _mybir.dt.from_np(a.dtype), kind="ExternalInput").ap())
    args.append(nc.dram_tensor("out_0", (N, D), F32, kind="ExternalOutput").ap())
    gnn_kernel(nc, *args)
    r = _run(nc, [arrays], core_ids=[0])
    return r.results[0]["out_0"]
```

```python
from contextlib import ExitStack

import concourse.bass as bass
from concourse import mybir

ALU = mybir.AluOpType
ACT = mybir.ActivationFunctionType
AX = mybir.AxisListType
F32 = mybir.dt.float32
F16 = mybir.dt.float16
BF16 = mybir.dt.bfloat16
I32 = mybir.dt.int32
ds = bass.ds

N = 50000
E = 50000
D = 64
RELS, BASES = 32, 8
P = 128
R = 4
GN = P * R
NG = -(-N // GN)
LASTP = (N - (NG - 1) * GN) // R
EP, ET = 125, 400
TG = 4
SG = ET // TG
NT = NG * TG
ES = NT // TG
STEPS = ES + NG - 1
PB = 4
W = D + 1
EPS = 1e-5
NB = NG // 2
BT = 2 * R
assert EP * ET == E and NT * P >= E and ES == NG and NB * 2 == NG and (N - (NG - 1) * GN) % R == 0


def gnn_kernel(nc, x, src, dst, etype, w1, b1, w2, b2, wg, bg, coeff, wb, hbias, loopw, out):
    with ExitStack() as ctx:
        def sb(name, shape, dt=F32):
            return ctx.enter_context(nc.sbuf_tensor(name, shape, dt))

        def ps(name, dt=F32, cols=512):
            return ctx.enter_context(nc.psum_tensor(name, [P, cols], dt))

        def sem(name):
            return ctx.enter_context(nc.semaphore(name))

        h_dram = nc.dram_tensor("h_rows", [N, D], F32)
        h1_dram = nc.dram_tensor("h1_rows", [N, 4 * D], BF16)
        x1_dram = nc.dram_tensor("x1_rows", [N, D], F32)

        T = sb("node_table", [P, NG, R, W])
        iota512 = sb("iota512", [P, GN], F16)
        iota16 = sb("iota16", [P, NT], F16)
        rel3 = sb("rel3", [P, 3 * RELS], F16)
        group_base = sb("group_base", [P, NG])
        ident = sb("ident", [P, P])
        ident16 = sb("ident16", [P, P], F16)
        identb = sb("identb", [P, P], BF16)
        tri = sb("tri", [P, P], F16)
        trc = sb("trc", [P, P], F16)
        ones16 = sb("ones16", [P, P], F16)
        ones32 = sb("ones32", [P, P])
        zero16 = sb("zero16", [P, 512], F16)
        eps = sb("eps", [P, 1])

        weighed = sb("weighed", [P, TG, BASES, D])
        early = weighed[:, :, :, :].rearrange("p u b f -> p (u b f)").bitcast(I32)
        e_src, e_dst, e_typ, e_tmp, e_tm2 = (early[0:EP, n * ET:(n + 1) * ET] for n in range(5))
        half = sb("half", [P, TG, BASES // 2, D])
        quarter = sb("quarter", [P, TG, BASES // 4, D])
        h16 = [sb(f"h16_{b}", [P, BT, 4 * D], BF16) for b in range(2)]
        x1b = [sb(f"x1b{b}", [P, BT, D]) for b in range(2)]
        hrest = sb("hrest", [P, BT, D])
        hbT = sb("hbT", [P, 512])
        half_flat = half[:, :, :, :].rearrange("p u b f -> p (u b f)")
        h16_flat = [h16[b][:, :, :].rearrange("p t f -> p (t f)").bitcast(F32) for b in range(2)]
        dec = [half_flat[:, 0:NT], half_flat[:, NT:2 * NT],
               quarter[:, :, :, :].rearrange("p u b f -> p (u b f)")[:, 0:NT]]
        dec_i = [hbT[:, 0:NT].bitcast(I32), sb("dec_i", [P, NT], I32)]
        part = [h16_flat[c // 2][0:EP, c % 2 * ET:(c % 2 + 1) * ET] for c in range(4)]
        place_hi, place_lo = (x1b[b][:, :, :].rearrange("p t f -> p (t f)")[0:EP, 0:ET] for b in range(2))
        pos_f = [hrest[:, :, :].rearrange("p t f -> p (t f)")[0:EP, 0:ET], sb("pos_f1", [EP, ET])]
        e_tm3 = sb("e_tm3", [EP, ET], I32)
        key = [sb(f"key{s}", [EP, ET]) for s in range(2)]
        kept_hot = T[:, :, :, :].rearrange("p g r w -> p (g r w)").bitcast(F16)[0:EP, 0:ET * NG]
        key_hot = [sb(f"key_hot{b}", [EP, TG * NG], F16) for b in range(2)]
        junk = sb("junk", [EP, 2 * TG, NG], F16)
        totals = sb("totals", [P, NG])
        starts = sb("starts", [P, NG])
        hi_hot = [sb(f"hi_hot{b}", [EP, NT], F16) for b in range(PB)]
        eq_hot = [sb(f"eq_hot{b}", [EP, P], F16) for b in range(PB)]
        lo_hot = [sb(f"lo_hot{b}", [EP, 4, P], F16) for b in range(PB)]
        node = [sb(f"segment_node{s}", [P, NT]) for s in range(2)]
        srt_src = [sb(f"sorted_src{s}", [P, NT], I32) for s in range(2)]
        srt_dst = sb("sorted_dst", [P, NT], I32)
        srt_typ = sb("sorted_typ", [P, NT])
        first_group = [sb(f"first_group{s}", [1, ES + 1], I32) for s in range(2)]

        idx = [sb(f"idx{b}", [P, 2, TG], I32) for b in range(2)]
        rows = [sb(f"rows{b}", [P, TG, 2, D]) for b in range(2)]
        rows16 = [rows[b][:, :, :, :].rearrange("p u e f -> p u (e f)").bitcast(BF16) for b in range(2)]
        rowsT = sb("rowsT", [P, TG * P])
        rows16T = rowsT[:, :].bitcast(BF16).rearrange("p (u h e) -> p u h e", u=TG, h=2)
        hidT = sb("hidT", [D + 1, TG * P])
        gate = sb("gate", [P, TG, D])
        msum = sb("message", [P, TG, D])
        mrest = sb("message_rest", [P, TG, D])
        msg_hi = [sb(f"msg_hi{b}", [P, TG, W], BF16) for b in range(2)]
        msg_mid = [sb(f"msg_mid{b}", [P, TG, D], BF16) for b in range(2)]
        msg_lo = [sb(f"msg_lo{b}", [P, TG, D], BF16) for b in range(2)]
        hot = [sb(f"hot{u}", [P, R, P], BF16) for u in range(TG)]
        rel_hot = sb("rel_hot", [P, TG, 3 * RELS], F16)
        rel_hotT = sb("rel_hotT", [3 * RELS, TG * P], BF16)
        cof = [sb(f"cof{b}", [P, TG, BASES]) for b in range(2)]

        xb = [sb(f"xb{b}", [P, BT, D]) for b in range(2)]
        hb = [sb(f"hb{b}", [P, BT, D]) for b in range(2)]
        cen = sb("cen", [P, BT, D])
        sq = sb("sq", [P, BT, D])
        st = sb("st", [P, 6, BT])

        w1s = sb("w1s", [2 * D, D])
        b1s = sb("b1s", [D, 1])
        w2s = sb("w2s", [D + 1, 2 * D])
        w2T = sb("w2T", [D, D + 1])
        wgs = sb("wgs", [D, D])
        bgs = sb("bgs", [D + 1, D])
        c3 = sb("c3", [3 * RELS, BASES])
        c3r = sb("c3r", [3 * RELS, BASES])
        c3b = [sb(f"c3b{k}", [3 * RELS, BASES], BF16) for k in range(3)]
        cpart = sb("cpart", [3 * RELS, BASES], BF16)
        wcat = sb("wcat", [P, BASES, D])
        wcat_r = sb("wcat_rest", [P, BASES, D])
        wparts = [sb(f"wcat_part{k}", [P, BASES, D], BF16) for k in range(3)]
        loop2 = sb("loop2", [P, P])
        hbias_s = sb("hbias_s", [P, D])

        pk = [ps(f"pk{i}") for i in range(4)]
        p_run = ps("p_run")
        p_tr = ps("p_tr")
        p_mm = ps("p_mm")
        p_out = ps("p_out")
        p_rel = p_mm[:, :].bitcast(F16)
        p_trb = p_tr[:, :].bitcast(BF16).rearrange("p (u h e) -> p u h e", u=TG, h=2)
        step_sum = p_run[:, 0:R * W].rearrange("p (r w) -> p r w", w=W)

        consts = sem("consts")
        loaded_edges = sem("loaded_edges")
        loaded_w = sem("loaded_w")
        vdone = sem("vector_done")
        wprep = sem("weights_prepared")
        w2_turned = sem("w2_turned")
        w2_copied = sem("w2_copied")
        w2_folded = sem("w2_folded")
        weights_ready = sem("weights_ready")
        kept_ready = sem("kept_hot_ready")
        key_ready = sem("key_hot_ready")
        key_used = [sem(f"key_hot_used{b}") for b in range(2)]
        counted = sem("groups_counted")
        starts_ready = sem("starts_ready")
        ranks_ready = [sem(f"ranks_ready{s}") for s in range(2)]
        ranks_read = [sem(f"ranks_read{s}") for s in range(2)]
        eq_ready = sem("eq_hot_ready")
        place_ready = sem("place_hot_ready")
        act_scaled = sem("lo_hot_scaled_by_act")
        pool_scaled = sem("lo_hot_scaled_by_pool")
        place_used = sem("place_hot_used")
        pieces_read = sem("pieces_read")
        x_loaded = [sem(f"x_loaded{b}") for b in range(2)]
        centred = sem("centred")
        squared = sem("squared")
        var_ready = sem("var_ready")
        dev_ready = sem("dev_ready")
        hb_ready = [sem(f"hb_ready{b}") for b in range(2)]
        hb_stored = [sem(f"hb_stored{b}") for b in range(2)]
        h1_turned = sem("h1_turned")
        h1_copied = sem("h1_copied")
        looped = sem("looped")
        loop_added = sem("loop_added")
        sorted_ready = sem("sorted_ready")
        idx_ready = [sem(f"idx_ready{b}") for b in range(2)]
        gathered = [sem(f"gathered{b}") for b in range(2)]
        gathers_started = sem("gathers_started")
        rows_turned = sem("rows_turned")
        turned_copied = sem("turned_copied")
        hid_ready = sem("hid_ready")
        hidT_ready = sem("hidT_ready")
        pre_ready = sem("pre_ready")
        gate_ready = sem("gate_ready")
        msum_ready = sem("message_ready")
        hi_ready = sem("hi_ready")
        rest_ready = sem("rest_ready")
        mid_ready = sem("mid_ready")
        msg_ready = sem("message_parts_ready")
        rel_ready = sem("rel_ready")
        rel_turned = sem("rel_turned")
        relT_ready = sem("relT_ready")
        cof_made = sem("cof_made")
        cof_ready = sem("cof_ready")
        edge_ready = sem("edge_products_ready")
        weighed_ready = sem("weighed_ready")
        half_ready = sem("half_ready")
        quarter_ready = sem("quarter_ready")
        hot_ready = sem("hot_ready")
        hot_used = sem("hot_used")
        h16_ready = [sem(f"h16_ready{b}") for b in range(2)]
        step_added = sem("step_added")
        out_ready = [sem(f"out_ready{b}") for b in range(2)]
        out_stored = [sem(f"out_stored{b}") for b in range(2)]

        block = ctx.enter_context(nc.Block())

        def blocks(ap):
            full = ap[0:(NG - 2) * GN, :].rearrange("(g p r) f -> g p (r f)", p=P, r=R)
            return full

        def block_dma(eng, dram, tile, q, load, signal):
            t = tile[:, :, :].rearrange("p (g r) f -> p g (r f)", g=2)
            if q is not None:
                d = blocks(dram)[ds(q * 2, 2)].rearrange("g p x -> p g x")
                pairs = [(d, t)]
            else:
                lo = (NG - 2) * GN
                d0 = dram[lo:lo + GN, :].rearrange("(p r) f -> p (r f)", r=R)
                d1 = dram[lo + GN:N, :].rearrange("(p r) f -> p (r f)", r=R)
                pairs = [(d0, t[:, 0, :]), (d1, t[0:LASTP, 1, :])]
            for d, s in pairs:
                a, b = (s, d) if load else (d, s)
                eng.dma_start(a, b).then_inc(signal, 16)

        PAIRS = (NB - 1) // 2
        assert PAIRS * 2 + 1 == NB

        def over_blocks(eng, body):
            body(0, 0, 0)
            body(1, 1, 0)
            with eng.Fori(1, PAIRS) as i:
                for b in range(2):
                    body(i * 2 + b, b, i)
            body(None, 0, PAIRS)

        def over_sets(eng, body):
            for s in range(2):
                body(s, s, 0)
            with eng.Fori(1, ES // 2 - 2) as i:
                for b in range(2):
                    body(i * 2 + b, b, i)
            for s in range(ES - 4, ES):
                body(s, s % 2, s // 2)

        def has(s, ahead):
            return not isinstance(s, int) or s + ahead < ES

        def wait(eng, signal, value):
            if not isinstance(value, int) or value > 0:
                eng.wait_ge(signal, value)

        def moved(q, uses):
            return (uses + 1) * 16 if q is not None else uses * 16 + 32

        def moved_pass(b):
            return PAIRS * 16 + (0 if b else 32)

        own = [0, 0, 0]

        def done(ins):
            ins.then_inc(vdone, 1)
            own[1] += 1
            nc.vector.wait_ge(vdone, own[0] + own[1])

        def loop_starts():
            own[2] = own[0] + own[1]

        def turn(i, per):
            own[0], own[1] = own[2] + i * per, 0

        def loop_ends(turns, per):
            assert own[1] == per, (own[1], per)
            own[0], own[1] = own[2] + turns * per, 0

        @block.sync
        def _(sp):
            for t, a in ((e_src, src), (e_dst, dst), (e_typ, etype)):
                sp.dma_start(t[:, :], a.rearrange("(p t) -> p t", p=EP)).then_inc(loaded_edges, 16)
            n = 0
            for t, a in ((w1s[:, :], w1), (b1s[:, :], b1.rearrange("(p o) -> p o", o=1)),
                         (w2s[0:D, 0:D], w2), (w2s[D:D + 1, 0:D], b2.rearrange("(o f) -> o f", o=1)),
                         (wgs[:, :], wg),
                         (c3[0:RELS, :], coeff), (c3[RELS:2 * RELS, :], coeff), (c3[2 * RELS:3 * RELS, :], coeff),
                         (wcat[0:D, :, :], wb.rearrange("b f o -> f b o")), (wcat[D:P, :, :], wb.rearrange("b f o -> f b o")),
                         (hbias_s[:, :], hbias.rearrange("(o f) -> o f", o=1).broadcast_to([P, D]))):
                sp.dma_start(t, a).then_inc(loaded_w, 16)
                n += 16
            sp.wait_ge(wprep, 3)
            sp.dma_start(loop2[0:D, 0:D], loopw).then_inc(loaded_w, 16)
            sp.dma_start(loop2[D:P, D:P], loopw).then_inc(loaded_w, 16)
            sp.dma_start(bgs[D:D + 1, :], bg.rearrange("(o f) -> o f", o=1)).then_inc(loaded_w, 16)

            def load(dram, read, before):
                def body(q, b, uses):
                    wait(sp, read[b], before * (PAIRS + 1 - b) + uses)
                    block_dma(sp, dram, xb[b], q, True, x_loaded[b])
                over_blocks(sp, body)

            load(x, hb_ready, 0)
            load(x, hb_ready, 1)
            for b in range(2):
                sp.wait_ge(hb_ready[b], 2 * (PAIRS + 1 - b))
                sp.wait_ge(hb_stored[b], 3 * moved_pass(b))
            load(x1_dram, out_ready, 0)

        @block.gpsimd
        def _(pool):
            nc.gpsimd.iota(iota512[:, :], [[1, R], [R, P]], base=0, channel_multiplier=0,
                           allow_small_or_imprecise_dtypes=True).then_inc(consts, 1)
            nc.gpsimd.iota(iota16[:, :], [[1, NT]], base=0, channel_multiplier=0,
                           allow_small_or_imprecise_dtypes=True).then_inc(consts, 1)
            nc.gpsimd.iota(rel3[:, :], [[0, 3], [1, RELS]], base=0, channel_multiplier=0,
                           allow_small_or_imprecise_dtypes=True).then_inc(consts, 1)
            nc.gpsimd.iota(group_base[:, :], [[GN, NG]], base=0, channel_multiplier=0,
                           allow_small_or_imprecise_dtypes=True).then_inc(consts, 1)
            nc.gpsimd.iota(ones32[:, :], [[1, P]], base=0, channel_multiplier=-1,
                           allow_small_or_imprecise_dtypes=True).then_inc(consts, 1)

            def store_h(q, b, uses):
                pool.wait_ge(hb_ready[b], uses + 1)
                block_dma(pool, h_dram, hb[b], q, False, hb_stored[b])
            over_blocks(pool, store_h)

            def scale_lo(s):
                with pool.Fori(0, ET // PB) as i:
                    for b in range(PB):
                        t = i * PB + b
                        pool.wait_ge(eq_ready, s * ET + t + 1)
                        nc.gpsimd.tensor_tensor(lo_hot[b][:, 2, :], eq_hot[b][:, :],
                                                part[2][:, ds(t, 1)].broadcast_to([EP, P]),
                                                ALU.mult).then_inc(pool_scaled, 1)
            scale_lo(0)
            scale_lo(1)

            def gather(layer, table, buf, s, b, i):
                pool.wait_ge(idx_ready[b], layer * (ES // 2) + i + 1)
                if not isinstance(s, int) or s >= 2:
                    pool.wait_ge(rows_turned, layer * ES + s - 1)
                pool.sem_inc(gathers_started, 1)
                for u in range(TG):
                    for e, dest in enumerate(buf(b, u)):
                        pool.indirect_dma_start(
                            out=dest, out_offset=None, in_=table[:, :],
                            in_offset=bass.IndirectOffsetOnAxis(ap=idx[b][:, e, u:u + 1], axis=0)
                        ).then_inc(gathered[b], 16)

            for b in range(2):
                pool.wait_ge(hb_stored[b], moved_pass(b))
            over_sets(pool, lambda s, b, i: gather(
                0, h_dram, lambda b, u: (rows[b][:, u, 0, :], rows[b][:, u, 1, :]), s, b, i))

            def store_x1h1(q, b, uses):
                pool.wait_ge(h16_ready[b], uses + 1)
                block_dma(pool, x1_dram, x1b[b], q, False, hb_stored[b])
                block_dma(pool, h1_dram, h16[b], q, False, hb_stored[b])
            over_blocks(pool, store_x1h1)
            for b in range(2):
                pool.wait_ge(hb_stored[b], 3 * moved_pass(b))
            pool.wait_ge(rows_turned, ES)

            def fold(s):
                pool.wait_ge(weighed_ready, s * TG + TG)
                nc.gpsimd.tensor_tensor(half[:, :, :, :].rearrange("p u b f -> p u (b f)"),
                                        weighed[:, :, 0:4, :].rearrange("p u b f -> p u (b f)"),
                                        weighed[:, :, 4:8, :].rearrange("p u b f -> p u (b f)"),
                                        ALU.add).then_inc(half_ready, 1)
                pool.wait_ge(half_ready, s + 1)
                nc.gpsimd.tensor_tensor(quarter[:, :, :, :].rearrange("p u b f -> p u (b f)"),
                                        half[:, :, 0:2, :].rearrange("p u b f -> p u (b f)"),
                                        half[:, :, 2:4, :].rearrange("p u b f -> p u (b f)"),
                                        ALU.add).then_inc(quarter_ready, 1)
                pool.wait_ge(quarter_ready, s + 1)
                if not isinstance(s, int) or s >= 1:
                    pool.wait_ge(msg_ready, ES + s)
                nc.gpsimd.tensor_tensor(msum[:, :, :], quarter[:, :, 0, :], quarter[:, :, 1, :],
                                        ALU.add).then_inc(msum_ready, 1)

            def gather_and_fold(s, b, i):
                if isinstance(s, int) and s < 2:
                    return
                gather(1, h1_dram, lambda b, u: (rows16[b][:, u, :],), s, b, i)
                fold(s - 2)
            for s in range(2):
                gather(1, h1_dram, lambda b, u: (rows16[b][:, u, :],), s, s, 0)
            over_sets(pool, gather_and_fold)
            fold(ES - 2)
            fold(ES - 1)

            def store_out(q, b, uses):
                pool.wait_ge(out_ready[b], uses + 1)
                block_dma(pool, out, hb[b], q, False, out_stored[b])
            over_blocks(pool, store_out)
            for b in range(2):
                pool.wait_ge(out_stored[b], moved_pass(b))

        @block.scalar
        def _(act):
            act.wait_ge(w2_turned, 1)
            nc.scalar.activation(w2T[:, :], p_tr[0:D, 0:D + 1], ACT.Copy).then_inc(w2_copied, 1)

            act.wait_ge(wprep, 3)
            def norm(base):
                def body(q, b, uses):
                    c = base + (uses * 2 + b if q is not None else NB - 1)
                    act.wait_ge(centred, c + 1)
                    nc.scalar.activation(sq[:, :, :], cen[:, :, :], ACT.Square).then_inc(squared, 1)
                    act.wait_ge(var_ready, c + 1)
                    nc.scalar.activation(st[:, 3, :], st[:, 2, :], ACT.Sqrt, bias=eps[:, 0:1],
                                         scale=1.0 / D).then_inc(dev_ready, 1)
                    if base:
                        act.wait_ge(h1_turned, c - NB + 1)
                        nc.scalar.activation(hbT[:, :], p_tr[:, :], ACT.Copy).then_inc(h1_copied, 1)
                return body
            over_blocks(act, norm(0))

            def scale_lo(s):
                with act.Fori(0, ET // PB) as i:
                    for b in range(PB):
                        t = i * PB + b
                        act.wait_ge(eq_ready, s * ET + t + 1)
                        for c in range(2):
                            m = nc.scalar.activation(lo_hot[b][:, c, :], eq_hot[b][:, :], ACT.Copy,
                                                     scale=part[c][:, ds(t, 1)])
                        m.then_inc(act_scaled, 1)
            scale_lo(0)
            scale_lo(1)

            def parts(layer, s, b):
                n = layer * ES + s
                act.wait_ge(msum_ready, n + 1)
                nc.scalar.activation(msg_hi[b][:, :, 0:D], msum[:, :, :], ACT.Copy).then_inc(hi_ready, 1)
                act.wait_ge(rest_ready, n + 1)
                nc.scalar.activation(msg_mid[b][:, :, :], mrest[:, :, :], ACT.Copy).then_inc(mid_ready, 1)

            def copy_turned(s):
                act.wait_ge(rows_turned, s + 1)
                nc.scalar.activation(rowsT[:, :], p_tr[:, :], ACT.Copy).then_inc(turned_copied, 1)

            def hidden(s):
                act.wait_ge(hid_ready, s + 1)
                nc.scalar.activation(hidT[0:D, :], p_mm[0:D, :], ACT.Relu, bias=b1s[:, 0:1]).then_inc(hidT_ready, 1)

            def gates(s):
                act.wait_ge(pre_ready, s + 1)
                nc.scalar.activation(gate[:, :, :], p_out[:, :].rearrange("p (u e f) -> p u e f", u=TG, e=2)[:, :, 1, :],
                                     ACT.Tanh, scale=0.5).then_inc(gate_ready, 1)

            def layer0(s, b, i):
                if has(s, 1):
                    hidden(s + 1)
                if has(s, 2):
                    copy_turned(s + 2)
                if has(s, 1):
                    gates(s + 1)
                    parts(0, s + 1, 1 - b)
            copy_turned(0)
            hidden(0)
            copy_turned(1)
            gates(0)
            parts(0, 0, 0)
            over_sets(act, layer0)

            over_blocks(act, norm(NB))

            def turned1(s, b):
                act.wait_ge(rel_turned, s + 1)
                nc.scalar.activation(rel_hotT[:, :], p_rel[0:3 * RELS, 0:TG * P], ACT.Copy).then_inc(relT_ready, 1)
                act.wait_ge(rows_turned, ES + s + 1)
                nc.scalar.activation(rows16T[:, :, :, :], p_trb, ACT.Copy).then_inc(turned_copied, 1)
                act.wait_ge(cof_made, s + 1)
                nc.scalar.activation(cof[b][:, :, :], p_out[:, 0:TG * BASES].rearrange("p (u b) -> p u b", u=TG),
                                     ACT.Copy).then_inc(cof_ready, 1)

            def layer1(s, b, i):
                if has(s, 2):
                    turned1(s + 2, b)
                if has(s, 1):
                    parts(1, s + 1, 1 - b)
            turned1(0, 0)
            turned1(1, 1)
            parts(1, 0, 0)
            over_sets(act, layer1)

        @block.tensor
        def _(pe):
            mm = nc.tensor.matmul
            pe.wait_ge(loaded_w, 14 * 16)
            pe.wait_ge(wprep, 3)
            nc.tensor.transpose(p_tr[0:D, 0:D + 1], w2s[:, 0:D], ident[0:D + 1, 0:D + 1]).then_inc(w2_turned, 1)
            pe.wait_ge(w2_copied, 1)
            mm(p_mm[0:D + 1, 0:D], w2T[:, :], wgs[:, :], start=True, stop=True).then_inc(w2_folded, 1)

            def zero(bank, cols):
                return mm(bank[:, 0:cols], zero16[0:EP, 0:P], zero16[0:EP, 0:cols], start=True, stop=False,
                          skip_group_check=True)

            def add(out_, lhsT, rhs):
                return mm(out_, lhsT, rhs, start=False, stop=False, skip_group_check=True)

            run = (p_run, p_tr)

            def source_keys(t):
                return lambda u: kept_hot[:, ds(t * (TG * NG) + u * NG, NG)], kept_hot[:, ds(t * (TG * NG), TG * NG)]

            def destination_keys(b):
                return lambda u: key_hot[b][:, u * NG:(u + 1) * NG], key_hot[b][:, :]

            def over_unsorted(body):
                for b in range(2):
                    body(b, b)
                with pe.Fori(1, SG // 2) as i:
                    for b in range(2):
                        body(i * 2 + b, b)

            def count(t, b):
                pe.wait_ge(kept_ready, t + 1)
                one, _ = source_keys(t)
                for u in range(TG):
                    add(run[0][:, 0:NG], ones16[0:EP, :], one(u))
                pe.wait_ge(key_ready, t + 1)
                one, _ = destination_keys(b)
                for u in range(TG):
                    m = add(run[1][:, 0:NG], ones16[0:EP, :], one(u))
                m.then_inc(key_used[b], 1)
            for s in range(2):
                zero(run[s], NG)
            over_unsorted(count)
            zero(p_mm, 1).then_inc(counted, 1)

            for s in range(2):
                pe.wait_ge(starts_ready, s + 1)
                for u in range(TG):
                    m = mm(run[s][:, u * NG:(u + 1) * NG], ones32[0:1, :], starts[0:1, :], start=(u == 0), stop=False,
                           skip_group_check=True)
                m.then_inc(counted, 1)

            def rank(s, keys):
                one, every = keys
                m = add(run[s][:, 0:TG * NG], tri[0:EP, :], every)
                for u in range(TG):
                    for v in range(u):
                        m = add(run[s][:, u * NG:(u + 1) * NG], ones16[0:EP, :], one(v))
                m.then_inc(ranks_ready[s], 1)

            def pass_on(s, keys, t):
                one, every = keys
                pe.wait_ge(ranks_read[s], t + 1)
                m = add(run[s][:, 0:TG * NG], trc[0:EP, :], every)
                for u in range(TG):
                    for v in range(u + 1, TG):
                        m = add(run[s][:, u * NG:(u + 1) * NG], ones16[0:EP, :], one(v))
                return m

            def ranks(t, b):
                rank(0, source_keys(t))
                if not isinstance(t, int) or t > 0:
                    pass_on(1, destination_keys(1 - b), t - 1).then_inc(key_used[1 - b], 1)
                pe.wait_ge(key_ready, SG + t + 1)
                rank(1, destination_keys(b))
                pass_on(0, source_keys(t), t)
            over_unsorted(ranks)

            def move(s):
                if s:
                    pe.wait_ge(pieces_read, s)
                for c in range(3 + s):
                    zero(pk[c], NT)
                with pe.Fori(0, ET // PB) as i:
                    for b in range(PB):
                        n = s * ET + i * PB + b
                        pe.wait_ge(place_ready, n + 1)
                        if s:
                            m = add(pk[3][:, 0:NT], lo_hot[b][:, 3, :], hi_hot[b][:, :])
                        pe.wait_ge(act_scaled, n + 1)
                        for c in range(2):
                            m = add(pk[c][:, 0:NT], lo_hot[b][:, c, :], hi_hot[b][:, :])
                        pe.wait_ge(pool_scaled, n + 1)
                        add(pk[2][:, 0:NT], lo_hot[b][:, 2, :], hi_hot[b][:, :]).then_inc(place_used, 1)
            move(0)
            move(1)
            pe.wait_ge(sorted_ready, 1)

            def steps(layer, s, b):
                g0 = pe.value_load(first_group[layer][0:1, ds(s, 1)], min_val=0, max_val=NG - 1)
                g1 = pe.value_load(first_group[layer][0:1, ds(s + 1, 1)], min_val=0, max_val=NG - 1)
                with pe.Fori(g0, g1 + 1) as g:
                    k = s + g + layer * STEPS
                    pe.wait_ge(msg_ready, layer * ES + s + 1)
                    pe.wait_ge(step_added, k + 1)
                    for u in range(TG):
                        pe.wait_ge(hot_ready, k * TG + u + 1)
                        for r in range(R):
                            for n, part in enumerate((msg_hi, msg_mid, msg_lo)):
                                w = W if n == 0 else D
                                m = mm(step_sum[:, r, 0:w], hot[u][:, r, :], part[b][:, u, :],
                                       start=(u == 0 and r == 0 and n == 0),
                                       stop=(u == TG - 1 and r == R - 1 and n == 2), skip_group_check=True)
                        m.then_inc(hot_used, 1)

            pe.sem_inc(step_added, 1)
            pe.wait_ge(weights_ready, 1)

            def turn0(s, b, i):
                pe.wait_ge(gathered[b], 2 * 16 * TG * (i + 1))
                wait(pe, turned_copied, s)
                for u in range(TG):
                    m = nc.tensor.transpose(p_tr[:, u * P:(u + 1) * P],
                                            rows[b][:, u, :, :].rearrange("p e f -> p (e f)"), ident[:, :])
                m.then_inc(rows_turned, 1)

            def hidden(s):
                pe.wait_ge(turned_copied, s + 1)
                mm(p_mm[0:D, :], w1s[:, :], rowsT[:, :], start=True, stop=True).then_inc(hid_ready, 1)

            def outputs(s):
                pe.wait_ge(hidT_ready, s + 1)
                wait(pe, msum_ready, s)
                for u in range(TG):
                    m = mm(p_out[:, u * P:(u + 1) * P], hidT[:, u * P:(u + 1) * P], w2s[:, :],
                           start=(u == 0), stop=(u == TG - 1), skip_group_check=True)
                m.then_inc(pre_ready, 1)

            def layer0(s, b, i):
                if has(s, 1):
                    hidden(s + 1)
                if has(s, 2):
                    turn0(s + 2, b, i + 1)
                if has(s, 1):
                    outputs(s + 1)
                steps(0, s, b)
            turn0(0, 0, 0)
            hidden(0)
            turn0(1, 1, 0)
            outputs(0)
            over_sets(pe, layer0)

            def loop_block(q, b, uses):
                c = uses * 2 + b if q is not None else NB - 1
                pe.wait_ge(hb_ready[b], (PAIRS + 1 - b) + uses + 1)
                wait(pe, h1_copied, c)
                for j in range(4):
                    m = nc.tensor.transpose(p_tr[:, j * P:(j + 1) * P],
                                            hb[b][:, 2 * j:2 * j + 2, :].rearrange("p t f -> p (t f)"), ident[:, :])
                m.then_inc(h1_turned, 1)
                pe.wait_ge(h1_copied, c + 1)
                wait(pe, loop_added, c)
                for j in range(4):
                    m = mm(p_out[:, j * P:(j + 1) * P], hbT[:, j * P:(j + 1) * P], loop2[:, :],
                           start=(j == 0), stop=(j == 3), skip_group_check=True)
                m.then_inc(looped, 1)
            over_blocks(pe, loop_block)

            def turn1(s, b, i):
                pe.wait_ge(rel_ready, s + 1)
                wait(pe, relT_ready, s)
                for u in range(TG):
                    m = nc.tensor.transpose(p_rel[0:3 * RELS, u * P:(u + 1) * P], rel_hot[:, u, :], ident16[:, :])
                m.then_inc(rel_turned, 1)
                pe.wait_ge(gathered[b], 16 * TG * (ES + i + 1))
                pe.wait_ge(turned_copied, ES + s)
                for u in range(TG):
                    for h in range(2):
                        m = nc.tensor.transpose(p_trb[:, u, h, :], rows16[b][:, u, h * P:(h + 1) * P], identb[:, :])
                m.then_inc(rows_turned, 1)
                pe.wait_ge(relT_ready, s + 1)
                wait(pe, cof_ready, s)
                for u in range(TG):
                    m = mm(p_out[:, u * BASES:(u + 1) * BASES], rel_hotT[:, u * P:(u + 1) * P], cpart[:, :],
                           start=(u == 0), stop=(u == TG - 1), skip_group_check=True)
                m.then_inc(cof_made, 1)

            def edges(s):
                pe.wait_ge(turned_copied, ES + s + 1)
                for u in range(TG):
                    wait(pe, weighed_ready, (s - 1) * TG + u + 1)
                    for n, (h, k) in enumerate(((0, 0), (0, 1), (1, 2))):
                        m = mm(pk[u][:, :], rows16T[:, u, h, :], wparts[k][:, :, :].rearrange("p b f -> p (b f)"),
                               start=(n == 0), stop=(n == 2))
                    m.then_inc(edge_ready, 1)

            def layer1(s, b, i):
                if has(s, 1):
                    edges(s + 1)
                if has(s, 2):
                    turn1(s + 2, b, i + 1)
                steps(1, s, b)
            turn1(0, 0, 0)
            edges(0)
            turn1(1, 1, 0)
            over_sets(pe, layer1)

        @block.vector
        def _(dve):
            v = nc.vector
            dve.wait_ge(consts, 5)
            v.tensor_scalar(tri[:, :], ones32[:, :], 0.0, None, ALU.is_gt).then_inc(vdone, 1)
            v.tensor_scalar(trc[:, :], ones32[:, :], 0.0, None, ALU.is_le).then_inc(vdone, 1)
            v.tensor_scalar(ident[:, :], ones32[:, :], 0.0, None, ALU.is_equal).then_inc(vdone, 1)
            v.tensor_scalar(ident16[:, :], ones32[:, :], 0.0, None, ALU.is_equal).then_inc(vdone, 1)
            dve.wait_ge(vdone, 4)
            own[1] = 4
            v.tensor_copy(identb[:, :], ident[:, :])
            done(v.memset(ones32[:, :], 1.0))
            v.memset(ones16[:, :], 1.0)
            v.memset(zero16[:, :], 0.0)
            v.memset(hidT[D:D + 1, :], 1.0)
            for b in range(2):
                v.memset(msg_hi[b][:, :, D:W], 1.0)
            for b in range(2):
                v.memset(xb[b][:, :, :], 0.0)
            v.memset(loop2[:, :], 0.0).then_inc(wprep, 1)
            v.memset(bgs[:, :], 0.0).then_inc(wprep, 1)
            v.memset(eps[:, :], EPS).then_inc(wprep, 1)

            dve.wait_ge(loaded_w, 14 * 16)
            dve.wait_ge(w2_folded, 1)
            v.tensor_scalar(w2s[:, 0:D], w2s[:, 0:D], 0.5, None, ALU.mult)
            v.tensor_tensor(w2s[:, D:2 * D], p_mm[0:D + 1, 0:D], bgs[:, :], ALU.add).then_inc(weights_ready, 1)
            done(v.tensor_copy(c3b[0][:, :], c3[:, :]))
            done(v.tensor_tensor(c3r[:, :], c3[:, :], c3b[0][:, :], ALU.subtract))
            done(v.tensor_copy(c3b[1][:, :], c3r[:, :]))
            done(v.tensor_tensor(c3[:, :], c3r[:, :], c3b[1][:, :], ALU.subtract))
            done(v.tensor_copy(c3b[2][:, :], c3[:, :]))
            for k in range(3):
                done(v.tensor_copy(cpart[k * RELS:(k + 1) * RELS, :], c3b[k][k * RELS:(k + 1) * RELS, :]))
            done(v.tensor_copy(wparts[0][:, :, :], wcat[:, :, :]))
            done(v.tensor_tensor(wcat_r[:, :, :], wcat[:, :, :], wparts[0][:, :, :], ALU.subtract))
            done(v.tensor_copy(wparts[1][:, :, :], wcat_r[:, :, :]))
            done(v.tensor_tensor(wparts[2][:, :, :], wcat_r[:, :, :], wparts[1][:, :, :], ALU.subtract))
            done(v.tensor_copy(wparts[2][0:D, :, :], wparts[0][0:D, :, :]))

            dve.wait_ge(loaded_edges, 48)
            done(v.tensor_scalar(e_tmp[:, :], e_src[:, :], 5, None, ALU.arith_shift_right))
            done(v.tensor_copy(part[0][:, :], e_tmp[:, :]))
            done(v.tensor_scalar(e_tmp[:, :], e_src[:, :], 31, 5, ALU.bitwise_and, ALU.logical_shift_left))
            done(v.tensor_scalar(e_tm2[:, :], e_dst[:, :], 11, None, ALU.arith_shift_right))
            done(v.tensor_tensor(e_tm3[:, :], e_tmp[:, :], e_tm2[:, :], ALU.bitwise_or))
            done(v.tensor_copy(part[1][:, :], e_tm3[:, :]))
            done(v.tensor_scalar(e_tmp[:, :], e_dst[:, :], 2047, None, ALU.bitwise_and))
            done(v.tensor_scalar(part[2][:, :], e_tmp[:, :], 1.0, None, ALU.add))
            done(v.tensor_copy(part[3][:, :], e_typ[:, :]))
            for k, e in enumerate((e_src, e_dst)):
                done(v.tensor_scalar(e_tmp[:, :], e[:, :], 9, None, ALU.arith_shift_right))
                done(v.tensor_copy(key[k][:, :], e_tmp[:, :]))

            def norm(X, H, c):
                done(v.tensor_reduce(st[:, 0, :], X, AX.X, ALU.add))
                done(v.tensor_scalar(st[:, 1, :], st[:, 0, :], 1.0 / D, None, ALU.mult))
                v.tensor_tensor(cen[:, :, :], X, st[:, 1, :].rearrange("p (t o) -> p t o", o=1).broadcast_to([P, BT, D]),
                                ALU.subtract).then_inc(centred, 1)
                dve.wait_ge(squared, c + 1)
                v.tensor_reduce(st[:, 2, :], sq[:, :, :], AX.X, ALU.add).then_inc(var_ready, 1)
                dve.wait_ge(dev_ready, c + 1)
                done(v.reciprocal(st[:, 4, :], st[:, 3, :]))
                return v.scalar_tensor_tensor(
                    out=H, in0=cen[:, :, :], scalar=0.0,
                    in1=st[:, 4, :].rearrange("p (t o) -> p t o", o=1).broadcast_to([P, BT, D]),
                    op0=ALU.max, op1=ALU.mult)

            def chained(body, per):
                body(0, 0, 0)
                body(1, 1, 0)
                loop_starts()
                with dve.Fori(1, PAIRS) as i:
                    for b in range(2):
                        turn((i - 1) * 2 + b, per)
                        body(i * 2 + b, b, i)
                loop_ends(2 * PAIRS - 2, per)
                body(None, 0, PAIRS)

            def first(q, b, uses):
                c = uses * 2 + b if q is not None else NB - 1
                dve.wait_ge(x_loaded[b], moved(q, uses))
                wait(dve, hb_stored[b], uses * 16)
                norm(xb[b][:, :, :], hb[b][:, :, :], c).then_inc(hb_ready[b], 1)
            chained(first, 3)

            def over_unsorted(body):
                for b in range(2):
                    body(b, b)
                with dve.Fori(1, SG // 2) as i:
                    for b in range(2):
                        body(i * 2 + b, b)

            def source_hots(t):
                for u in range(TG):
                    m = v.tensor_scalar(kept_hot[:, ds(t * (TG * NG) + u * NG, NG)], iota16[0:EP, 0:NG],
                                        key[0][:, ds(t * TG + u, 1)], None, ALU.is_equal)
                m.then_inc(kept_ready, 1)

            def destination_hots(t, b, i):
                dve.wait_ge(key_used[b], i)
                for u in range(TG):
                    m = v.tensor_scalar(key_hot[b][:, u * NG:(u + 1) * NG], iota16[0:EP, 0:NG],
                                        key[1][:, ds(t * TG + u, 1)], None, ALU.is_equal)
                m.then_inc(key_ready, 1)

            for b in range(2):
                dve.sem_inc(key_used[b], 1)
            for b in range(2):
                source_hots(b)
                destination_hots(b, b, 1)
            with dve.Fori(1, SG // 2) as i:
                for b in range(2):
                    source_hots(i * 2 + b)
                    destination_hots(i * 2 + b, b, i + 1)
            for s in range(2):
                dve.wait_ge(counted, s + 1)
                done(v.tensor_copy(totals[:, :], (p_run, p_tr)[s][:, 0:NG]))
                done(v.tensor_tensor_scan(starts[:, :], ones32[:, 0:NG], totals[:, :], 0.0, ALU.mult, ALU.add))
                v.tensor_tensor(starts[:, :], starts[:, :], totals[:, :], ALU.subtract).then_inc(starts_ready, 1)

            def places(s, t, hots):
                dve.wait_ge(ranks_ready[s], t + 1)
                if not isinstance(t, int) or t > 0:
                    dve.wait_ge(ranks_read[s], t)
                for u in range(TG):
                    m = v.scalar_tensor_tensor(out=junk[:, s * TG + u, :], in0=(p_run, p_tr)[s][0:EP, u * NG:(u + 1) * NG],
                                               scalar=1.0, in1=hots(u), op0=ALU.mult, op1=ALU.mult,
                                               accum_out=pos_f[s][:, ds(t * TG + u, 1)])
                m.then_inc(ranks_read[s], 1)

            def ranked(t, b, i):
                destination_hots(t, b, SG // 2 + i + 1)
                if not isinstance(t, int) or t > 0:
                    places(1, t - 1, lambda u: key_hot[1 - b][:, u * NG:(u + 1) * NG])
                places(0, t, lambda u: kept_hot[:, ds(t * (TG * NG) + u * NG, NG)])
            dve.wait_ge(key_ready, SG)
            for b in range(2):
                ranked(b, b, 0)
            with dve.Fori(1, SG // 2) as i:
                for b in range(2):
                    ranked(i * 2 + b, b, i)
            places(1, SG - 1, lambda u: key_hot[1][:, u * NG:(u + 1) * NG])

            def sort(s):
                dve.wait_ge(ranks_read[s], SG)
                done(v.tensor_copy(e_tmp[:, :], pos_f[s][:, :]))
                done(v.tensor_scalar(e_tm2[:, :], e_tmp[:, :], 7, None, ALU.arith_shift_right))
                done(v.tensor_scalar(e_tm3[:, :], e_tmp[:, :], P - 1, None, ALU.bitwise_and))
                done(v.tensor_copy(place_hi[:, :], e_tm2[:, :]))
                done(v.tensor_copy(place_lo[:, :], e_tm3[:, :]))
                with dve.Fori(0, ET // PB) as i:
                    for b in range(PB):
                        t = i * PB + b
                        dve.wait_ge(place_used, s * ET + t + 1)
                        v.tensor_scalar(eq_hot[b][:, :], iota16[0:EP, 0:P], place_lo[:, ds(t, 1)], None,
                                        ALU.is_equal).then_inc(eq_ready, 1)
                        m = v.tensor_scalar(hi_hot[b][:, :], iota16[0:EP, :], place_hi[:, ds(t, 1)], None, ALU.is_equal)
                        if s:
                            m = v.tensor_scalar(lo_hot[b][:, 3, :], iota16[0:EP, 0:P], place_lo[:, ds(t, 1)],
                                                part[3][:, ds(t, 1)], ALU.is_equal, ALU.mult)
                        m.then_inc(place_ready, 1)
                dve.wait_ge(place_used, (s + 1) * ET + PB)
                done(v.tensor_copy(dec_i[0][:, :], pk[1][:, 0:NT]))
                done(v.tensor_scalar(dec_i[1][:, :], dec_i[0][:, :], 5, None, ALU.arith_shift_right))
                done(v.tensor_copy(dec[0][:, :], dec_i[1][:, :]))
                done(v.scalar_tensor_tensor(out=dec[1][:, :], in0=pk[0][:, 0:NT], scalar=32.0, in1=dec[0][:, :],
                                            op0=ALU.mult, op1=ALU.add))
                done(v.tensor_copy(srt_src[s][:, 0:NT], dec[1][:, :]))
                done(v.tensor_scalar(dec_i[1][:, :], dec_i[0][:, :], 31, None, ALU.bitwise_and))
                done(v.tensor_copy(dec[0][:, :], dec_i[1][:, :]))
                done(v.tensor_scalar(dec[2][:, :], pk[2][:, 0:NT], -1.0, 0.0, ALU.add, ALU.max))
                done(v.scalar_tensor_tensor(out=dec[2][:, :], in0=dec[0][:, :], scalar=2048.0, in1=dec[2][:, :],
                                            op0=ALU.mult, op1=ALU.add))
                if s == 0:
                    done(v.tensor_copy(srt_dst[:, 0:NT], dec[2][:, :]))
                else:
                    done(v.tensor_copy(srt_typ[:, :], pk[3][:, 0:NT]))
                seg = dec[1] if s == 0 else dec[2]
                done(v.tensor_copy(dec_i[0][0:1, :], seg[0:1, :]))
                done(v.tensor_scalar(dec_i[1][0:1, :], dec_i[0][0:1, :], 9, None, ALU.arith_shift_right))
                done(v.tensor_copy(first_group[s][0:1, 0:ES],
                                   dec_i[1][0:1, :].rearrange("p (s u) -> p s u", u=TG)[:, :, 0]))
                done(v.memset(first_group[s][0:1, 0:1], 0))
                done(v.memset(first_group[s][0:1, ES:ES + 1], NG - 1))
                done(v.tensor_scalar(dec[0][:, :], pk[2][:, 0:NT], 0.0, -65536.0, ALU.is_equal, ALU.mult))
                v.tensor_tensor(node[s][:, :], seg[:, :], dec[0][:, :], ALU.add).then_inc(pieces_read, 1)
                dve.wait_ge(pieces_read, s + 1)

            def put_idx(layer, s, b):
                m = v.tensor_copy(idx[b][:, 0, :], srt_src[layer][:, ds(s * TG, TG)])
                if layer == 0:
                    m = v.tensor_copy(idx[b][:, 1, :], srt_dst[:, ds(s * TG, TG)])
                m.then_inc(idx_ready[b], 1)

            dve.sem_inc(place_used, PB)
            sort(0)
            for b in range(2):
                put_idx(0, b, b)
            sort(1)
            v.memset(T[:, :, :, :], 0.0).then_inc(sorted_ready, 1)
            dve.wait_ge(sorted_ready, 1)

            def steps(layer, s):
                g0 = dve.value_load(first_group[layer][0:1, ds(s, 1)], min_val=0, max_val=NG - 1)
                g1 = dve.value_load(first_group[layer][0:1, ds(s + 1, 1)], min_val=0, max_val=NG - 1)
                with dve.Fori(g0, g1 + 1) as g:
                    k = s + g + layer * STEPS
                    for u in range(TG):
                        dve.wait_ge(hot_used, k * TG + u + 1)
                        v.tensor_scalar(hot[u][:, :, :].rearrange("p r n -> p (r n)"), iota512[:, :],
                                        group_base[:, ds(g, 1)], node[layer][:, ds(s * TG + u, 1)],
                                        ALU.add, ALU.is_equal).then_inc(hot_ready, 1)
                    dve.wait_ge(hot_used, (k + 2) * TG)
                    dve.wait_ge(step_added, k + 1)
                    tg = T[:, ds(g, 1), :, :].rearrange("p g r w -> p (g r w)")
                    v.tensor_tensor(tg, tg, p_run[:, 0:R * W], ALU.add).then_inc(step_added, 1)

            def next_idx(layer, s, b, i):
                if has(s, 2):
                    per = 32 * TG if layer == 0 else 16 * TG
                    dve.wait_ge(gathered[b], layer * 16 * TG * ES + per * (i + 2))
                    if has(s, 4):
                        put_idx(layer, s + 4, b)
                    elif layer == 0:
                        put_idx(1, s + 4 - ES, b)

            def parts(layer, s, b):
                n = layer * ES + s
                dve.wait_ge(hi_ready, n + 1)
                v.tensor_tensor(mrest[:, :, :], msum[:, :, :], msg_hi[b][:, :, 0:D], ALU.subtract).then_inc(rest_ready, 1)
                dve.wait_ge(mid_ready, n + 1)
                v.tensor_tensor(msg_lo[b][:, :, :], mrest[:, :, :], msg_mid[b][:, :, :], ALU.subtract).then_inc(msg_ready, 1)

            dve.sem_inc(hot_used, TG)
            def message(s):
                dve.wait_ge(gate_ready, s + 1)
                v.scalar_tensor_tensor(out=msum[:, :, :], in0=gate[:, :, :], scalar=1.0,
                                       in1=p_out[:, :].rearrange("p (u e f) -> p u e f", u=TG, e=2)[:, :, 0, :],
                                       op0=ALU.add, op1=ALU.mult).then_inc(msum_ready, 1)

            def layer0(s, b, i):
                steps(0, s)
                next_idx(0, s, b, i)
                if has(s, 1):
                    message(s + 1)
                    parts(0, s + 1, 1 - b)
            for b in range(2):
                next_idx(0, b - 2, b, -1)
            message(0)
            parts(0, 0, 0)
            over_sets(dve, layer0)

            def second(q, b, uses):
                c = uses * 2 + b if q is not None else NB - 1
                Tb = (T[:, ds(q * 2, 2), :, :] if q is not None else T[:, NG - 2:NG, :, :]).rearrange("p g r w -> p (g r) w")
                dve.wait_ge(x_loaded[b], moved(q, uses) + moved_pass(b))
                dve.wait_ge(hb_stored[b], uses * 32 + moved_pass(b))
                done(v.tensor_scalar(st[:, 0, :], Tb[:, :, D:W].rearrange("p t w -> p (t w)"), 1.0, None, ALU.max))
                done(v.reciprocal(st[:, 1, :], st[:, 0, :]))
                done(v.tensor_tensor(cen[:, :, :], Tb[:, :, 0:D],
                                     st[:, 1, :].rearrange("p (t o) -> p t o", o=1).broadcast_to([P, BT, D]), ALU.mult))
                done(v.tensor_tensor(x1b[b][:, :, :], xb[b][:, :, :], cen[:, :, :], ALU.add))
                norm(x1b[b][:, :, :], hb[b][:, :, :], NB + c).then_inc(hb_ready[b], 1)
                dve.wait_ge(hb_ready[b], PAIRS + 1 - b + uses + 1)
                v.tensor_copy(h16[b][:, :, 3 * D:4 * D], hb[b][:, :, :])
                done(v.tensor_copy(h16[b][:, :, 0:D], hb[b][:, :, :]))
                done(v.tensor_tensor(hrest[:, :, :], hb[b][:, :, :], h16[b][:, :, 0:D], ALU.subtract))
                done(v.tensor_copy(h16[b][:, :, D:2 * D], hrest[:, :, :]))
                v.tensor_tensor(h16[b][:, :, 2 * D:3 * D], hrest[:, :, :], h16[b][:, :, D:2 * D],
                                ALU.subtract).then_inc(h16_ready[b], 1)
                dve.wait_ge(looped, c + 1)
                v.tensor_tensor(Tb[:, :, 0:D], p_out[:, :].rearrange("p (t f) -> p t f", f=D),
                                hbias_s[:, :].rearrange("p (o f) -> p o f", o=1).broadcast_to([P, BT, D]),
                                ALU.add).then_inc(loop_added, 1)
            dve.wait_ge(step_added, STEPS + 1)
            chained(second, 10)
            dve.wait_ge(loop_added, NB)

            def relations(s):
                wait(dve, rel_turned, s)
                for u in range(TG):
                    m = v.tensor_scalar(rel_hot[:, u, :], rel3[:, :], srt_typ[:, ds(s * TG + u, 1)], None, ALU.is_equal)
                m.then_inc(rel_ready, 1)

            def weigh(s, b):
                dve.wait_ge(cof_ready, s + 1)
                wait(dve, half_ready, s)
                for u in range(TG):
                    dve.wait_ge(edge_ready, s * TG + u + 1)
                    v.tensor_tensor(weighed[:, u, :, :], pk[u][:, :].rearrange("p (b f) -> p b f", b=BASES),
                                    cof[b][:, u, :].rearrange("p (b o) -> p b o", o=1).broadcast_to([P, BASES, D]),
                                    ALU.mult).then_inc(weighed_ready, 1)

            def layer1(s, b, i):
                if has(s, 2):
                    relations(s + 2)
                if has(s, 1):
                    weigh(s + 1, 1 - b)
                steps(1, s)
                next_idx(1, s, b, i)
                if has(s, 1):
                    parts(1, s + 1, 1 - b)
            for s in range(2):
                relations(s)
            for b in range(2):
                next_idx(1, b - 2, b, -1)
            weigh(0, 0)
            parts(1, 0, 0)
            over_sets(dve, layer1)
            dve.wait_ge(step_added, 2 * STEPS + 1)

            def third(q, b, uses):
                Tb = (T[:, ds(q * 2, 2), :, :] if q is not None else T[:, NG - 2:NG, :, :]).rearrange("p g r w -> p (g r) w")
                dve.wait_ge(x_loaded[b], moved(q, uses) + 2 * moved_pass(b))
                wait(dve, out_stored[b], uses * 16)
                v.scalar_tensor_tensor(out=hb[b][:, :, :], in0=Tb[:, :, 0:D], scalar=0.0, in1=xb[b][:, :, :],
                                       op0=ALU.max, op1=ALU.add).then_inc(out_ready[b], 1)
            over_blocks(dve, third)


_INS = ['x', 'src', 'dst', 'edge_type_32', 'L0_gnn_W1', 'L0_gnn_b1', 'L0_gnn_W2', 'L0_gnn_b2', 'L0_gnn_Wg', 'L0_gnn_bg',
        'L1_gnn_coeff', 'L1_gnn_W', 'L1_gnn_h_bias', 'L1_gnn_loop_weight']


def kernel(**inputs):
    import numpy as _np
    import concourse.bacc as _bacc
    from concourse import mybir as _mybir
    from concourse.bass_utils import run_bass_kernel_spmd as _run

    nc = _bacc.Bacc("TRN2", target_bir_lowering=False, num_devices=1)
    arrays, args = {}, []
    for name in _INS:
        a = _np.ascontiguousarray(inputs[name])
        arrays[f"in_{name}"] = a
        args.append(nc.dram_tensor(f"in_{name}", a.shape, _mybir.dt.from_np(a.dtype), kind="ExternalInput").ap())
    args.append(nc.dram_tensor("out_0", (N, D), F32, kind="ExternalOutput").ap())
    gnn_kernel(nc, *args)
    r = _run(nc, [arrays], core_ids=[0])
    return r.results[0]["out_0"]
```

```python
from contextlib import ExitStack

import concourse.bass as bass
from concourse import mybir

ALU = mybir.AluOpType
ACT = mybir.ActivationFunctionType
AX = mybir.AxisListType
F32 = mybir.dt.float32
F16 = mybir.dt.float16
BF16 = mybir.dt.bfloat16
I32 = mybir.dt.int32
ds = bass.ds

N = 50000
E = 50000
D = 64
RELS, BASES = 32, 8
P = 128
R = 4
GN = P * R
NG = -(-N // GN)
LASTP = (N - (NG - 1) * GN) // R
EP, ET = 125, 400
TG = 4
SG = ET // TG
NT = NG * TG
ES = NT // TG
STEPS = ES + NG - 1
PB = 4
W = D + 1
EPS = 1e-5
NB = NG // 2
BT = 2 * R
assert EP * ET == E and NT * P >= E and ES == NG and NB * 2 == NG and (N - (NG - 1) * GN) % R == 0


def gnn_kernel(nc, x, src, dst, etype, w1, b1, w2, b2, wg, bg, coeff, wb, hbias, loopw, out):
    with ExitStack() as ctx:
        def sb(name, shape, dt=F32):
            return ctx.enter_context(nc.sbuf_tensor(name, shape, dt))

        def ps(name, dt=F32, cols=512):
            return ctx.enter_context(nc.psum_tensor(name, [P, cols], dt))

        def sem(name):
            return ctx.enter_context(nc.semaphore(name))

        h_dram = nc.dram_tensor("h_rows", [N, D], F32)
        h1_dram = nc.dram_tensor("h1_rows", [N, 4 * D], BF16)
        x1_dram = nc.dram_tensor("x1_rows", [N, D], F32)

        T = sb("node_table", [P, NG, R, W])
        iota512 = sb("iota512", [P, GN], F16)
        iota16 = sb("iota16", [P, NT], F16)
        rel3 = sb("rel3", [P, 3 * RELS], F16)
        group_base = sb("group_base", [P, NG])
        ident = sb("ident", [P, P])
        ident16 = sb("ident16", [P, P], F16)
        identb = sb("identb", [P, P], BF16)
        tri = sb("tri", [P, P], F16)
        trc = sb("trc", [P, P], F16)
        ones16 = sb("ones16", [P, P], F16)
        ones32 = sb("ones32", [P, P])
        zero16 = sb("zero16", [P, 512], F16)
        eps = sb("eps", [P, 1])

        weighed = sb("weighed", [P, TG, BASES, D])
        early = weighed[:, :, :, :].rearrange("p u b f -> p (u b f)").bitcast(I32)
        e_src, e_dst, e_typ, e_tmp, e_tm2 = (early[0:EP, n * ET:(n + 1) * ET] for n in range(5))
        half = sb("half", [P, TG, BASES // 2, D])
        quarter = sb("quarter", [P, TG, BASES // 4, D])
        h16 = [sb(f"h16_{b}", [P, BT, 4 * D], BF16) for b in range(2)]
        x1b = [sb(f"x1b{b}", [P, BT, D]) for b in range(2)]
        hrest = sb("hrest", [P, BT, D])
        sq = sb("sq", [P, BT, D])
        hbT = sb("hbT", [P, 512])
        half_flat = half[:, :, :, :].rearrange("p u b f -> p (u b f)")
        h16_flat = [h16[b][:, :, :].rearrange("p t f -> p (t f)").bitcast(F32) for b in range(2)]
        dec = [half_flat[:, 0:NT], half_flat[:, NT:2 * NT],
               quarter[:, :, :, :].rearrange("p u b f -> p (u b f)")[:, 0:NT]]
        dec_i = [hbT[:, 0:NT].bitcast(I32), sb("dec_i", [P, NT], I32)]
        part = [h16_flat[c // 2][0:EP, c % 2 * ET:(c % 2 + 1) * ET] for c in range(4)]
        place_hi, place_lo = (x1b[b][:, :, :].rearrange("p t f -> p (t f)")[0:EP, 0:ET] for b in range(2))
        pos_f = [hrest[:, :, :].rearrange("p t f -> p (t f)")[0:EP, 0:ET], sq[:, :, :].rearrange("p t f -> p (t f)")[0:EP, 0:ET]]
        e_tm3 = sb("e_tm3", [EP, ET], I32)
        key = [sb(f"key{s}", [EP, ET]) for s in range(2)]
        kept_hot = T[:, :, :, :].rearrange("p g r w -> p (g r w)").bitcast(F16)[0:EP, 0:ET * NG]
        key_hot = [sb(f"key_hot{b}", [EP, TG * NG], F16) for b in range(2)]
        junk = sb("junk", [EP, 2 * TG, NG], F16)
        totals = sb("totals", [P, NG])
        starts = sb("starts", [P, NG])
        hi_hot = [sb(f"hi_hot{b}", [EP, NT], F16) for b in range(PB)]
        eq_hot = [sb(f"eq_hot{b}", [EP, P], F16) for b in range(PB)]
        lo_hot = [sb(f"lo_hot{b}", [EP, 4, P], F16) for b in range(PB)]
        node = [sb(f"segment_node{s}", [P, NT]) for s in range(2)]
        srt_src = [sb(f"sorted_src{s}", [P, NT], I32) for s in range(2)]
        srt_dst = sb("sorted_dst", [P, NT], I32)
        srt_typ = sb("sorted_typ", [P, NT])
        first_group = [sb(f"first_group{s}", [1, ES + 1], I32) for s in range(2)]

        idx = [sb(f"idx{b}", [P, 2, TG], I32) for b in range(2)]
        rows = [sb(f"rows{b}", [P, TG, 2, D]) for b in range(2)]
        rows16 = [rows[b][:, :, :, :].rearrange("p u e f -> p u (e f)").bitcast(BF16) for b in range(2)]
        rowsT = sb("rowsT", [P, TG * P])
        pooled = rows[0][:, :, :, :].rearrange("p u e f -> p (u e) f")
        rows16T = rowsT[:, :].bitcast(BF16).rearrange("p (u h e) -> p u h e", u=TG, h=2)
        hidT = sb("hidT", [D + 1, TG * P])
        gate = sb("gate", [P, TG, D])
        msum = sb("message", [P, TG, D])
        mrest = sb("message_rest", [P, TG, D])
        msg_hi = [sb(f"msg_hi{b}", [P, TG, W], BF16) for b in range(2)]
        msg_mid = [sb(f"msg_mid{b}", [P, TG, D], BF16) for b in range(2)]
        msg_lo = [sb(f"msg_lo{b}", [P, TG, D], BF16) for b in range(2)]
        hot = [sb(f"hot{u}", [P, R, P], BF16) for u in range(TG)]
        rel_hot = sb("rel_hot", [P, TG, 3 * RELS], F16)
        rel_hotT = sb("rel_hotT", [3 * RELS, TG * P], BF16)
        cof = [sb(f"cof{b}", [P, TG, BASES]) for b in range(2)]

        xb = [sb(f"xb{b}", [P, BT, D]) for b in range(2)]
        hb = [sb(f"hb{b}", [P, BT, D]) for b in range(2)]
        cen = sb("cen", [P, BT, D])
        x1_in = [*xb, *x1b]
        out_of = [*hb, cen, sq]
        st = [sb(f"st{b}", [P, 7, BT]) for b in range(2)]

        w1s = sb("w1s", [2 * D, D])
        b1s = sb("b1s", [D, 1])
        w2s = sb("w2s", [D + 1, 2 * D])
        w2T = sb("w2T", [D, D + 1])
        wgs = sb("wgs", [D, D])
        bgs = sb("bgs", [D + 1, D])
        c3 = sb("c3", [3 * RELS, BASES])
        c3r = sb("c3r", [3 * RELS, BASES])
        c3b = [sb(f"c3b{k}", [3 * RELS, BASES], BF16) for k in range(3)]
        cpart = sb("cpart", [3 * RELS, BASES], BF16)
        wcat = sb("wcat", [P, BASES, D])
        wcat_r = sb("wcat_rest", [P, BASES, D])
        wparts = [sb(f"wcat_part{k}", [P, BASES, D], BF16) for k in range(3)]
        loop2 = sb("loop2", [P, P])
        hbias_s = sb("hbias_s", [1, D])
        hbias_r = sb("hbias_rest", [1, D])
        hbias3 = [sb(f"hbias_part{k}", [1, D], BF16) for k in range(3)]
        onesb = sb("onesb", [1, P], BF16)

        pk = [ps(f"pk{i}") for i in range(4)]
        p_run = ps("p_run")
        p_tr = ps("p_tr")
        p_mm = ps("p_mm")
        p_out = ps("p_out")
        p_rel = p_mm[:, :].bitcast(F16)
        p_trb = p_tr[:, :].bitcast(BF16).rearrange("p (u h e) -> p u h e", u=TG, h=2)
        step_sum = p_run[:, 0:R * W].rearrange("p (r w) -> p r w", w=W)

        consts = sem("consts")
        loaded_edges = sem("loaded_edges")
        loaded_w = sem("loaded_w")
        vdone = sem("vector_done")
        wprep = sem("weights_prepared")
        w2_turned = sem("w2_turned")
        w2_copied = sem("w2_copied")
        w2_folded = sem("w2_folded")
        weights_ready = sem("weights_ready")
        kept_ready = sem("kept_hot_ready")
        key_ready = sem("key_hot_ready")
        key_used = [sem(f"key_hot_used{b}") for b in range(2)]
        counted = sem("groups_counted")
        starts_ready = sem("starts_ready")
        ranks_ready = [sem(f"ranks_ready{s}") for s in range(2)]
        ranks_read = [sem(f"ranks_read{s}") for s in range(2)]
        eq_ready = sem("eq_hot_ready")
        place_ready = sem("place_hot_ready")
        act_scaled = sem("lo_hot_scaled_by_act")
        pool_scaled = sem("lo_hot_scaled_by_pool")
        place_used = sem("place_hot_used")
        pieces_read = sem("pieces_read")
        x_loaded = [sem(f"x_loaded{b}") for b in range(2)]
        centred = sem("centred")
        squared = sem("squared")
        var_ready = sem("var_ready")
        dev_ready = sem("dev_ready")
        hb_ready = [sem(f"hb_ready{b}") for b in range(2)]
        hb_stored = [sem(f"hb_stored{b}") for b in range(2)]
        x1_ready = sem("x1_ready")
        x1_stored = [sem(f"x1_stored{b}") for b in range(2)]
        counts_inverted = sem("counts_inverted")
        pooled_ready = sem("pooled_ready")
        hi16_ready = sem("h1_high_ready")
        hi16_twice = sem("h1_high_twice")
        rest16_ready = sem("h1_rest_ready")
        mid16_ready = sem("h1_middle_ready")
        lo16_ready = sem("h1_low_ready")
        h1_turned = sem("h1_turned")
        h1_copied = sem("h1_copied")
        looped = sem("looped")
        loop_added = sem("loop_added")
        sorted_ready = sem("sorted_ready")
        table_cleared = sem("table_cleared")
        idx_ready = [sem(f"idx_ready{b}") for b in range(2)]
        gathered = [sem(f"gathered{b}") for b in range(2)]
        gathers_started = sem("gathers_started")
        rows_turned = sem("rows_turned")
        turned_copied = sem("turned_copied")
        hid_ready = sem("hid_ready")
        hidT_ready = sem("hidT_ready")
        pre_ready = sem("pre_ready")
        gate_ready = sem("gate_ready")
        msum_ready = sem("message_ready")
        hi_ready = sem("hi_ready")
        rest_ready = sem("rest_ready")
        mid_ready = sem("mid_ready")
        msg_ready = sem("message_parts_ready")
        rel_ready = sem("rel_ready")
        rel_turned = sem("rel_turned")
        relT_ready = sem("relT_ready")
        cof_made = sem("cof_made")
        cof_ready = sem("cof_ready")
        edge_ready = sem("edge_products_ready")
        weighed_ready = sem("weighed_ready")
        half_ready = sem("half_ready")
        quarter_ready = sem("quarter_ready")
        hot_ready = sem("hot_ready")
        hot_used = sem("hot_used")
        h16_stored = [sem(f"h16_stored{b}") for b in range(2)]
        step_added = sem("step_added")
        step_cleared = sem("step_cleared")
        x1_loaded = [sem(f"x1_loaded{b}") for b in range(4)]
        out_ready = sem("out_ready")
        out_stored = [sem(f"out_stored{b}") for b in range(4)]

        block = ctx.enter_context(nc.Block())

        def blocks(ap):
            full = ap[0:(NG - 2) * GN, :].rearrange("(g p r) f -> g p (r f)", p=P, r=R)
            return full

        def block_dma(eng, dram, tile, q, load, signal):
            t = tile[:, :, :].rearrange("p (g r) f -> p g (r f)", g=2)
            if q is not None:
                d = blocks(dram)[ds(q * 2, 2)].rearrange("g p x -> p g x")
                pairs = [(d, t)]
            else:
                lo = (NG - 2) * GN
                d0 = dram[lo:lo + GN, :].rearrange("(p r) f -> p (r f)", r=R)
                d1 = dram[lo + GN:N, :].rearrange("(p r) f -> p (r f)", r=R)
                pairs = [(d0, t[:, 0, :]), (d1, t[0:LASTP, 1, :])]
            for d, s in pairs:
                a, b = (s, d) if load else (d, s)
                eng.dma_start(a, b).then_inc(signal, 16)

        PAIRS = (NB - 1) // 2
        assert PAIRS * 2 + 1 == NB

        def over_blocks(eng, body):
            body(0, 0, 0)
            body(1, 1, 0)
            with eng.Fori(1, PAIRS) as i:
                for b in range(2):
                    body(i * 2 + b, b, i)
            body(None, 0, PAIRS)

        def groups_of(engine, layer, s):
            _, (g0, g1) = nc.values_load_multi_w_load_instructions(
                first_group[layer][0:1, ds(s, 2)], engines=[engine], min_val=0, max_val=NG - 1)
            return g0, g1

        def act_pieces(s, b):
            return 1 if s == 0 and b == 0 else 2

        def over_fours(body, eng):
            for b in range(4):
                body(b, b, 0)
            with eng.Fori(1, NB // 4) as i:
                for b in range(4):
                    body(i * 4 + b, b, i)
            body(NB - 1, 0, NB // 4)
        assert NB // 4 * 4 + 1 == NB

        def over_turns(eng, body, last):
            for c in range(4):
                body(c, c % 2, c // 2)
            with eng.Fori(2, PAIRS - 1) as i:
                for b in range(2):
                    body(i * 2 + b, b, i)
            for c in range(2 * PAIRS - 2, last + 1):
                body(c, c % 2, c // 2)

        def within(c):
            return not isinstance(c, int) or 0 <= c < NB

        def name_of(c):
            return None if isinstance(c, int) and c == NB - 1 else c

        def over_sets(eng, body):
            for s in range(2):
                body(s, s, 0)
            with eng.Fori(1, ES // 2 - 2) as i:
                for b in range(2):
                    body(i * 2 + b, b, i)
            for s in range(ES - 4, ES):
                body(s, s % 2, s // 2)

        def has(s, ahead):
            return not isinstance(s, int) or s + ahead < ES

        def wait(eng, signal, value):
            if not isinstance(value, int) or value > 0:
                eng.wait_ge(signal, value)

        def moved(q, uses):
            return (uses + 1) * 16 if q is not None else uses * 16 + 32

        def moved_pass(b):
            return PAIRS * 16 + (0 if b else 32)

        def block_of(table, c):
            return table[:, ds(c * 2, 2), :, :].rearrange("p g r w -> p (g r) w")

        own = [0, 0, 0]

        def done(ins):
            nc.vector.wait_ge(vdone, begun(ins))

        def begun(ins):
            ins.then_inc(vdone, 1)
            own[1] += 1
            return own[0] + own[1]

        def loop_starts():
            own[2] = own[0] + own[1]

        def turn(i, per):
            own[0], own[1] = own[2] + i * per, 0

        def loop_ends(turns, per):
            assert own[1] == per, (own[1], per)
            own[0], own[1] = own[2] + turns * per, 0

        @block.sync
        def _(sp):
            for t, a in ((e_src, src), (e_dst, dst), (e_typ, etype)):
                sp.dma_start(t[:, :], a.rearrange("(p t) -> p t", p=EP)).then_inc(loaded_edges, 16)
            n = 0
            for t, a in ((w1s[:, :], w1), (b1s[:, :], b1.rearrange("(p o) -> p o", o=1)),
                         (w2s[0:D, 0:D], w2), (w2s[D:D + 1, 0:D], b2.rearrange("(o f) -> o f", o=1)),
                         (wgs[:, :], wg),
                         (c3[0:RELS, :], coeff), (c3[RELS:2 * RELS, :], coeff), (c3[2 * RELS:3 * RELS, :], coeff),
                         (wcat[0:D, :, :], wb.rearrange("b f o -> f b o")), (wcat[D:P, :, :], wb.rearrange("b f o -> f b o")),
                         (hbias_s[:, :], hbias.rearrange("(o f) -> o f", o=1))):
                sp.dma_start(t, a).then_inc(loaded_w, 16)
                n += 16
            sp.wait_ge(wprep, 3)
            sp.dma_start(loop2[0:D, 0:D], loopw).then_inc(loaded_w, 16)
            sp.dma_start(loop2[D:P, D:P], loopw).then_inc(loaded_w, 16)
            sp.dma_start(bgs[D:D + 1, :], bg.rearrange("(o f) -> o f", o=1)).then_inc(loaded_w, 16)

            def load(dram, c, b):
                block_dma(sp, dram, xb[b], name_of(c), True, x_loaded[b])

            for b in range(2):
                load(x, b, b)

            def first(c, b, uses):
                if within(c + 2):
                    sp.wait_ge(centred, c + 1)
                    load(x, c + 2, b)
                if within(c - 1):
                    sp.wait_ge(hb_ready[1 - b], uses + b)
                    block_dma(sp, h_dram, hb[1 - b], name_of(c - 1), False, hb_stored[1 - b])
            over_turns(sp, first, NB)

            sp.wait_ge(centred, NB)
            for b in range(2):
                load(x, b, b)

            def second(c, b, uses):
                if within(c):
                    sp.wait_ge(x1_ready, c + 1)
                    if within(c + 2):
                        load(x, c + 2, b)
                    block_dma(sp, x1_dram, x1b[b], name_of(c), False, x1_stored[b])
                if within(c - 2):
                    sp.wait_ge(hi16_twice, c - 1)
                    sp.wait_ge(lo16_ready, c - 1)
                    block_dma(sp, h1_dram, h16[b], name_of(c - 2), False, h16_stored[b])
            over_turns(sp, second, NB + 1)

            for b in range(2):
                sp.wait_ge(x1_stored[b], moved_pass(b))

            def load_x1(q, b, uses):
                if not isinstance(q, int) or q >= 4:
                    sp.wait_ge(out_ready, q - 3)
                block_dma(sp, x1_dram, x1_in[b], name_of(q), True, x1_loaded[b])
            over_fours(load_x1, sp)

        @block.gpsimd
        def _(pool):
            nc.gpsimd.iota(iota512[:, :], [[1, R], [R, P]], base=0, channel_multiplier=0,
                           allow_small_or_imprecise_dtypes=True).then_inc(consts, 1)
            nc.gpsimd.iota(iota16[:, :], [[1, NT]], base=0, channel_multiplier=0,
                           allow_small_or_imprecise_dtypes=True).then_inc(consts, 1)
            nc.gpsimd.iota(rel3[:, :], [[0, 3], [1, RELS]], base=0, channel_multiplier=0,
                           allow_small_or_imprecise_dtypes=True).then_inc(consts, 1)
            nc.gpsimd.iota(group_base[:, :], [[GN, NG]], base=0, channel_multiplier=0,
                           allow_small_or_imprecise_dtypes=True).then_inc(consts, 1)
            nc.gpsimd.iota(ones32[:, :], [[1, P]], base=0, channel_multiplier=-1,
                           allow_small_or_imprecise_dtypes=True).then_inc(consts, 1)

            def scale_lo(s):
                with pool.Fori(0, ET // PB) as i:
                    for b in range(PB):
                        t = i * PB + b
                        pool.wait_ge(eq_ready, s * ET + t + 1)
                        nc.gpsimd.tensor_tensor(lo_hot[b][:, 2, :], eq_hot[b][:, :],
                                                part[2][:, ds(t, 1)].broadcast_to([EP, P]),
                                                ALU.mult).then_inc(pool_scaled, 1)
            def clear_table(half_):
                nc.gpsimd.memset(T[:, half_ * (NG // 2):(half_ + 1) * (NG // 2), :, :], 0.0).then_inc(table_cleared, 1)
            scale_lo(0)
            clear_table(0)
            scale_lo(1)

            def gather(layer, table, buf, s, b, i):
                pool.wait_ge(idx_ready[b], layer * (ES // 2) + i + 1)
                if not isinstance(s, int) or s >= 2:
                    pool.wait_ge(rows_turned, layer * ES + s - 1)
                pool.sem_inc(gathers_started, 1)
                for u in range(TG):
                    for e, dest in enumerate(buf(b, u)):
                        pool.indirect_dma_start(
                            out=dest, out_offset=None, in_=table[:, :],
                            in_offset=bass.IndirectOffsetOnAxis(ap=idx[b][:, e, u:u + 1], axis=0)
                        ).then_inc(gathered[b], 16)

            for b in range(2):
                pool.wait_ge(hb_stored[b], moved_pass(b))

            def gather0(s, b, i):
                gather(0, h_dram, lambda b, u: (rows[b][:, u, 0, :], rows[b][:, u, 1, :]), s, b, i)
                if isinstance(s, int) and s == 1:
                    clear_table(1)
            over_sets(pool, gather0)

            def mean_of_messages(c, b):
                pool.wait_ge(counts_inverted, c + 1)
                wait(pool, x1_ready, c)
                nc.gpsimd.tensor_tensor(
                    pooled, block_of(T, c)[:, :, 0:D],
                    st[b][:, 6, :].rearrange("p (t o) -> p t o", o=1).broadcast_to([P, BT, D]),
                    ALU.mult).then_inc(pooled_ready, 1)

            def second(c, b, uses):
                o = 1 - b
                if within(c + 1):
                    mean_of_messages(c + 1, o)
                if within(c - 1):
                    pool.wait_ge(hi16_ready, c)
                    wait(pool, lo16_ready, c - 1)
                    nc.gpsimd.tensor_tensor(hrest[:, :, :], hb[o][:, :, :], h16[o][:, :, 0:D],
                                            ALU.subtract).then_inc(rest16_ready, 1)
                    pool.wait_ge(rest16_ready, c)
                    pool.wait_ge(mid16_ready, c)
                    nc.gpsimd.tensor_tensor(h16[o][:, :, 2 * D:3 * D], hrest[:, :, :], h16[o][:, :, D:2 * D],
                                            ALU.subtract).then_inc(lo16_ready, 1)
            pool.wait_ge(rows_turned, ES)
            mean_of_messages(0, 0)
            over_turns(pool, second, NB)
            for b in range(2):
                pool.wait_ge(h16_stored[b], moved_pass(b))

            def fold(s):
                for h in range(2):
                    u2 = slice(h * TG // 2, (h + 1) * TG // 2)
                    pool.wait_ge(weighed_ready, s * TG + (h + 1) * TG // 2)
                    if h == 0:
                        wait(pool, quarter_ready, s)
                    nc.gpsimd.tensor_tensor(half[:, u2, :, :].rearrange("p u b f -> p u (b f)"),
                                            weighed[:, u2, 0:4, :].rearrange("p u b f -> p u (b f)"),
                                            weighed[:, u2, 4:8, :].rearrange("p u b f -> p u (b f)"),
                                            ALU.add).then_inc(half_ready, 1)
                pool.wait_ge(half_ready, 2 * s + 2)
                pool.wait_ge(msum_ready, ES + s)
                nc.gpsimd.tensor_tensor(quarter[:, :, :, :].rearrange("p u b f -> p u (b f)"),
                                        half[:, :, 0:2, :].rearrange("p u b f -> p u (b f)"),
                                        half[:, :, 2:4, :].rearrange("p u b f -> p u (b f)"),
                                        ALU.add).then_inc(quarter_ready, 1)

            def gather_and_fold(s, b, i):
                if isinstance(s, int) and s < 2:
                    return
                gather(1, h1_dram, lambda b, u: (rows16[b][:, u, :],), s, b, i)
                fold(s - 2)
            for s in range(2):
                gather(1, h1_dram, lambda b, u: (rows16[b][:, u, :],), s, s, 0)
            over_sets(pool, gather_and_fold)
            fold(ES - 2)
            fold(ES - 1)

            def store_out(q, b, uses):
                pool.wait_ge(out_ready, q + 1)
                block_dma(pool, out, out_of[b], name_of(q), False, out_stored[b])
            over_fours(store_out, pool)
            for b in range(4):
                pool.wait_ge(out_stored[b], NB // 4 * 16 + (0 if b else 32))

        @block.scalar
        def _(act):
            act.wait_ge(w2_turned, 1)
            nc.scalar.activation(w2T[:, :], p_tr[0:D, 0:D + 1], ACT.Copy).then_inc(w2_copied, 1)

            act.wait_ge(wprep, 3)
            def norm(base):
                def body(c, b, uses):
                    o = 1 - b
                    if within(c - 1):
                        act.wait_ge(var_ready, base + c)
                        nc.scalar.activation(st[o][:, 3, :], st[o][:, 2, :], ACT.Sqrt, bias=eps[:, 0:1],
                                             scale=1.0 / D).then_inc(dev_ready, 1)
                    if base and within(c - 1):
                        act.wait_ge(hb_ready[o], PAIRS + 1 - o + uses + b)
                        nc.scalar.activation(h16[o][:, :, 0:D], hb[o][:, :, :], ACT.Copy).then_inc(hi16_ready, 1)
                    if within(c):
                        act.wait_ge(centred, base + c + 1)
                        centre = cen if base or b == 0 else x1b[0]
                        nc.scalar.activation(sq[:, :, :], centre[:, :, :], ACT.Square).then_inc(squared, 1)
                    if base and within(c - 2):
                        act.wait_ge(looped, c - 1)
                        nc.scalar.activation(block_of(T, c - 2)[:, :, 0:D],
                                             p_out[:, :].rearrange("p (t f) -> p t f", f=D), ACT.Copy).then_inc(loop_added, 1)
                    if base and within(c - 1):
                        act.wait_ge(h1_turned, c)
                        nc.scalar.activation(hbT[:, :], p_tr[:, :], ACT.Copy).then_inc(h1_copied, 1)
                        act.wait_ge(rest16_ready, c)
                        nc.scalar.activation(h16[o][:, :, D:2 * D], hrest[:, :, :], ACT.Copy).then_inc(mid16_ready, 1)
                return body
            over_turns(act, norm(0), NB)

            def scale_lo(s):
                with act.Fori(0, ET // PB) as i:
                    for b in range(PB):
                        t = i * PB + b
                        act.wait_ge(eq_ready, s * ET + t + 1)
                        for c in range(act_pieces(s, b)):
                            m = nc.scalar.activation(lo_hot[b][:, c, :], eq_hot[b][:, :], ACT.Copy,
                                                     scale=part[c][:, ds(t, 1)])
                        m.then_inc(act_scaled, 1)
            scale_lo(0)
            scale_lo(1)

            def parts(layer, s, b):
                n = layer * ES + s
                act.wait_ge(msum_ready, n + 1)
                nc.scalar.activation(msg_hi[b][:, :, 0:D], msum[:, :, :], ACT.Copy).then_inc(hi_ready, 1)
                act.wait_ge(rest_ready, n + 1)
                nc.scalar.activation(msg_mid[b][:, :, :], mrest[:, :, :], ACT.Copy).then_inc(mid_ready, 1)

            def copy_turned(s):
                act.wait_ge(rows_turned, s + 1)
                nc.scalar.activation(rowsT[:, :], p_tr[:, :], ACT.Copy).then_inc(turned_copied, 1)

            def hidden(s):
                act.wait_ge(hid_ready, s + 1)
                nc.scalar.activation(hidT[0:D, :], p_mm[0:D, :], ACT.Relu, bias=b1s[:, 0:1]).then_inc(hidT_ready, 1)

            def gates(s):
                act.wait_ge(pre_ready, s + 1)
                nc.scalar.activation(gate[:, :, :], p_out[:, :].rearrange("p (u e f) -> p u e f", u=TG, e=2)[:, :, 1, :],
                                     ACT.Tanh, scale=0.5).then_inc(gate_ready, 1)

            def layer0(s, b, i):
                if has(s, 1):
                    hidden(s + 1)
                if has(s, 2):
                    copy_turned(s + 2)
                if has(s, 1):
                    gates(s + 1)
                    parts(0, s + 1, 1 - b)
            copy_turned(0)
            hidden(0)
            copy_turned(1)
            gates(0)
            parts(0, 0, 0)
            over_sets(act, layer0)

            over_turns(act, norm(NB), NB + 1)

            def turned1(s, b):
                act.wait_ge(rel_turned, s + 1)
                nc.scalar.activation(rel_hotT[:, :], p_rel[0:3 * RELS, 0:TG * P], ACT.Copy).then_inc(relT_ready, 1)
                act.wait_ge(rows_turned, ES + s + 1)
                nc.scalar.activation(rows16T[:, :, :, :], p_trb, ACT.Copy).then_inc(turned_copied, 1)
                act.wait_ge(cof_made, s + 1)
                nc.scalar.activation(cof[b][:, :, :], p_out[:, 0:TG * BASES].rearrange("p (u b) -> p u b", u=TG),
                                     ACT.Copy).then_inc(cof_ready, 1)

            def layer1(s, b, i):
                if has(s, 2):
                    turned1(s + 2, b)
                if has(s, 1):
                    parts(1, s + 1, 1 - b)
            turned1(0, 0)
            turned1(1, 1)
            parts(1, 0, 0)
            over_sets(act, layer1)

        @block.tensor
        def _(pe):
            mm = nc.tensor.matmul
            pe.wait_ge(loaded_w, 14 * 16)
            pe.wait_ge(wprep, 3)
            nc.tensor.transpose(p_tr[0:D, 0:D + 1], w2s[:, 0:D], ident[0:D + 1, 0:D + 1]).then_inc(w2_turned, 1)
            pe.wait_ge(w2_copied, 1)
            mm(p_mm[0:D + 1, 0:D], w2T[:, :], wgs[:, :], start=True, stop=True).then_inc(w2_folded, 1)

            def zero(bank, cols):
                return mm(bank[:, 0:cols], zero16[0:EP, 0:P], zero16[0:EP, 0:cols], start=True, stop=False,
                          skip_group_check=True)

            def add(out_, lhsT, rhs):
                return mm(out_, lhsT, rhs, start=False, stop=False, skip_group_check=True)

            run = (p_run, p_tr)

            def source_keys(t):
                return lambda u: kept_hot[:, ds(t * (TG * NG) + u * NG, NG)], kept_hot[:, ds(t * (TG * NG), TG * NG)]

            def destination_keys(b):
                return lambda u: key_hot[b][:, u * NG:(u + 1) * NG], key_hot[b][:, :]

            def over_unsorted(body):
                for b in range(2):
                    body(b, b)
                with pe.Fori(1, SG // 2) as i:
                    for b in range(2):
                        body(i * 2 + b, b)

            def count(t, b):
                pe.wait_ge(kept_ready, t + 1)
                one, _ = source_keys(t)
                for u in range(TG):
                    add(run[0][:, 0:NG], ones16[0:EP, :], one(u))
                pe.wait_ge(key_ready, t + 1)
                one, _ = destination_keys(b)
                for u in range(TG):
                    m = add(run[1][:, 0:NG], ones16[0:EP, :], one(u))
                m.then_inc(key_used[b], 1)
            for s in range(2):
                zero(run[s], NG)
            over_unsorted(count)
            zero(p_mm, 1).then_inc(counted, 1)

            for s in range(2):
                pe.wait_ge(starts_ready, s + 1)
                for u in range(TG):
                    m = mm(run[s][:, u * NG:(u + 1) * NG], ones32[0:1, :], starts[0:1, :], start=(u == 0), stop=False,
                           skip_group_check=True)
                m.then_inc(counted, 1)

            def rank(s, keys):
                one, every = keys
                m = add(run[s][:, 0:TG * NG], tri[0:EP, :], every)
                for u in range(TG):
                    for v in range(u):
                        m = add(run[s][:, u * NG:(u + 1) * NG], ones16[0:EP, :], one(v))
                m.then_inc(ranks_ready[s], 1)

            def pass_on(s, keys, t):
                one, every = keys
                pe.wait_ge(ranks_read[s], t + 1)
                m = add(run[s][:, 0:TG * NG], trc[0:EP, :], every)
                for u in range(TG):
                    for v in range(u + 1, TG):
                        m = add(run[s][:, u * NG:(u + 1) * NG], ones16[0:EP, :], one(v))
                return m

            def ranks(t, b):
                rank(0, source_keys(t))
                if not isinstance(t, int) or t > 0:
                    pass_on(1, destination_keys(1 - b), t - 1).then_inc(key_used[1 - b], 1)
                pe.wait_ge(key_ready, SG + t + 1)
                rank(1, destination_keys(b))
                pass_on(0, source_keys(t), t)
            over_unsorted(ranks)

            def move(s):
                if s:
                    pe.wait_ge(pieces_read, s)
                for c in range(3 + s):
                    zero(pk[c], NT)
                with pe.Fori(0, ET // PB) as i:
                    for b in range(PB):
                        n = s * ET + i * PB + b
                        pe.wait_ge(place_ready, n + 1)
                        if s:
                            m = add(pk[3][:, 0:NT], lo_hot[b][:, 3, :], hi_hot[b][:, :])
                        pe.wait_ge(act_scaled, n + 1)
                        for c in range(2):
                            m = add(pk[c][:, 0:NT], lo_hot[b][:, c, :], hi_hot[b][:, :])
                        pe.wait_ge(pool_scaled, n + 1)
                        add(pk[2][:, 0:NT], lo_hot[b][:, 2, :], hi_hot[b][:, :]).then_inc(place_used, 1)
            move(0)
            move(1)
            pe.wait_ge(sorted_ready, 1)

            def steps(layer, s, b):
                g0, g1 = groups_of(mybir.EngineType.PE, layer, s)
                with pe.Fori(g0, g1 + 1) as g:
                    k = s + g + layer * STEPS
                    made = pe.snap(k * TG)
                    free = pe.snap(k + layer + 2)
                    pe.wait_ge(msg_ready, layer * ES + s + 1)
                    pe.wait_ge(hot_ready, made + 1)
                    pe.wait_ge(step_added, free)
                    for u in range(TG):
                        if u > 0:
                            pe.wait_ge(hot_ready, made + u + 1)
                        for r in range(R):
                            for n, part in enumerate((msg_hi, msg_mid, msg_lo)):
                                w = W if n == 0 else D
                                m = mm(step_sum[:, r, 0:w], hot[u][:, r, :], part[b][:, u, :],
                                       start=(u == 0 and r == 0 and n == 0),
                                       stop=(u == TG - 1 and r == R - 1 and n == 2), skip_group_check=True)
                        m.then_inc(hot_used, 1)

            def clear_step(layer):
                wait(pe, step_added, layer * (STEPS + 2))
                mm(p_run[:, 0:R * W], zero16[:, 0:P], zero16[:, 0:R * W], start=True, stop=True).then_inc(step_cleared, 1)

            pe.sem_inc(step_added, 1)
            clear_step(0)
            pe.wait_ge(weights_ready, 1)

            def turn0(s, b, i):
                pe.wait_ge(gathered[b], 2 * 16 * TG * (i + 1))
                wait(pe, turned_copied, s)
                for u in range(TG):
                    m = nc.tensor.transpose(p_tr[:, u * P:(u + 1) * P],
                                            rows[b][:, u, :, :].rearrange("p e f -> p (e f)"), ident[:, :])
                m.then_inc(rows_turned, 1)

            def hidden(s):
                pe.wait_ge(turned_copied, s + 1)
                mm(p_mm[0:D, :], w1s[:, :], rowsT[:, :], start=True, stop=True).then_inc(hid_ready, 1)

            def outputs(s):
                pe.wait_ge(hidT_ready, s + 1)
                wait(pe, msum_ready, s)
                for u in range(TG):
                    m = mm(p_out[:, u * P:(u + 1) * P], hidT[:, u * P:(u + 1) * P], w2s[:, :],
                           start=(u == 0), stop=(u == TG - 1), skip_group_check=True)
                m.then_inc(pre_ready, 1)

            def layer0(s, b, i):
                if has(s, 1):
                    hidden(s + 1)
                if has(s, 2):
                    turn0(s + 2, b, i + 1)
                if has(s, 1):
                    outputs(s + 1)
                steps(0, s, b)
            turn0(0, 0, 0)
            hidden(0)
            turn0(1, 1, 0)
            outputs(0)
            over_sets(pe, layer0)

            def loop_block(q, b, uses):
                c = uses * 2 + b if q is not None else NB - 1
                pe.wait_ge(hb_ready[b], (PAIRS + 1 - b) + uses + 1)
                wait(pe, h1_copied, c)
                for j in range(4):
                    m = nc.tensor.transpose(p_tr[:, j * P:(j + 1) * P],
                                            hb[b][:, 2 * j:2 * j + 2, :].rearrange("p t f -> p (t f)"), ident[:, :])
                m.then_inc(h1_turned, 1)
                wait(pe, loop_added, c)
                for k in range(3):
                    mm(p_out[:, :], onesb[0:1, :], hbias3[k][0:1, :].rearrange("p (o f) -> p o f", o=1).broadcast_to([1, BT, D]),
                       start=(k == 0), stop=False, skip_group_check=True)
                pe.wait_ge(h1_copied, c + 1)
                for j in range(4):
                    m = mm(p_out[:, j * P:(j + 1) * P], hbT[:, j * P:(j + 1) * P], loop2[:, :],
                           start=False, stop=(j == 3), skip_group_check=True)
                m.then_inc(looped, 1)
            over_blocks(pe, loop_block)

            def turn1(s, b, i):
                pe.wait_ge(rel_ready, 2 * s + 2)
                wait(pe, relT_ready, s)
                for u in range(TG):
                    m = nc.tensor.transpose(p_rel[0:3 * RELS, u * P:(u + 1) * P], rel_hot[:, u, :], ident16[:, :])
                m.then_inc(rel_turned, 1)
                pe.wait_ge(gathered[b], 16 * TG * (ES + i + 1))
                pe.wait_ge(turned_copied, ES + s)
                for u in range(TG):
                    for h in range(2):
                        m = nc.tensor.transpose(p_trb[:, u, h, :], rows16[b][:, u, h * P:(h + 1) * P], identb[:, :])
                m.then_inc(rows_turned, 1)
                pe.wait_ge(relT_ready, s + 1)
                wait(pe, cof_ready, s)
                for u in range(TG):
                    m = mm(p_out[:, u * BASES:(u + 1) * BASES], rel_hotT[:, u * P:(u + 1) * P], cpart[:, :],
                           start=(u == 0), stop=(u == TG - 1), skip_group_check=True)
                m.then_inc(cof_made, 1)

            def edges(s):
                pe.wait_ge(turned_copied, ES + s + 1)
                for u in range(TG):
                    wait(pe, weighed_ready, (s - 1) * TG + u + 1)
                    for n, (h, k) in enumerate(((0, 0), (0, 1), (1, 2))):
                        m = mm(pk[u][:, :], rows16T[:, u, h, :], wparts[k][:, :, :].rearrange("p b f -> p (b f)"),
                               start=(n == 0), stop=(n == 2))
                    m.then_inc(edge_ready, 1)

            def layer1(s, b, i):
                if has(s, 1):
                    edges(s + 1)
                if has(s, 2):
                    turn1(s + 2, b, i + 1)
                steps(1, s, b)
            clear_step(1)
            turn1(0, 0, 0)
            edges(0)
            turn1(1, 1, 0)
            over_sets(pe, layer1)

        @block.vector
        def _(dve):
            v = nc.vector
            dve.wait_ge(consts, 5)
            v.tensor_scalar(tri[:, :], ones32[:, :], 0.0, None, ALU.is_gt).then_inc(vdone, 1)
            v.tensor_scalar(trc[:, :], ones32[:, :], 0.0, None, ALU.is_le).then_inc(vdone, 1)
            v.tensor_scalar(ident[:, :], ones32[:, :], 0.0, None, ALU.is_equal).then_inc(vdone, 1)
            v.tensor_scalar(ident16[:, :], ones32[:, :], 0.0, None, ALU.is_equal).then_inc(vdone, 1)
            dve.wait_ge(vdone, 4)
            own[1] = 4
            v.tensor_copy(identb[:, :], ident[:, :])
            done(v.memset(ones32[:, :], 1.0))
            v.memset(ones16[:, :], 1.0)
            v.memset(zero16[:, :], 0.0)
            v.memset(onesb[:, :], 1.0)
            v.memset(hidT[D:D + 1, :], 1.0)
            for b in range(2):
                v.memset(msg_hi[b][:, :, D:W], 1.0)
            for b in range(2):
                v.memset(xb[b][:, :, :], 0.0)
            v.memset(loop2[:, :], 0.0).then_inc(wprep, 1)
            v.memset(bgs[:, :], 0.0).then_inc(wprep, 1)
            v.memset(eps[:, :], EPS).then_inc(wprep, 1)

            dve.wait_ge(loaded_w, 14 * 16)
            dve.wait_ge(w2_folded, 1)
            v.tensor_scalar(w2s[:, 0:D], w2s[:, 0:D], 0.5, None, ALU.mult)
            v.tensor_tensor(w2s[:, D:2 * D], p_mm[0:D + 1, 0:D], bgs[:, :], ALU.add).then_inc(weights_ready, 1)
            done(v.tensor_copy(c3b[0][:, :], c3[:, :]))
            done(v.tensor_tensor(c3r[:, :], c3[:, :], c3b[0][:, :], ALU.subtract))
            done(v.tensor_copy(c3b[1][:, :], c3r[:, :]))
            done(v.tensor_tensor(c3[:, :], c3r[:, :], c3b[1][:, :], ALU.subtract))
            done(v.tensor_copy(c3b[2][:, :], c3[:, :]))
            for k in range(3):
                done(v.tensor_copy(cpart[k * RELS:(k + 1) * RELS, :], c3b[k][k * RELS:(k + 1) * RELS, :]))
            done(v.tensor_copy(hbias3[0][:, :], hbias_s[:, :]))
            done(v.tensor_tensor(hbias_r[:, :], hbias_s[:, :], hbias3[0][:, :], ALU.subtract))
            done(v.tensor_copy(hbias3[1][:, :], hbias_r[:, :]))
            done(v.tensor_tensor(hbias3[2][:, :], hbias_r[:, :], hbias3[1][:, :], ALU.subtract))
            done(v.tensor_copy(wparts[0][:, :, :], wcat[:, :, :]))
            done(v.tensor_tensor(wcat_r[:, :, :], wcat[:, :, :], wparts[0][:, :, :], ALU.subtract))
            done(v.tensor_copy(wparts[1][:, :, :], wcat_r[:, :, :]))
            done(v.tensor_tensor(wparts[2][:, :, :], wcat_r[:, :, :], wparts[1][:, :, :], ALU.subtract))
            done(v.tensor_copy(wparts[2][0:D, :, :], wparts[0][0:D, :, :]))

            dve.wait_ge(loaded_edges, 48)
            done(v.tensor_scalar(e_tmp[:, :], e_src[:, :], 5, None, ALU.arith_shift_right))
            done(v.tensor_copy(part[0][:, :], e_tmp[:, :]))
            done(v.tensor_scalar(e_tmp[:, :], e_src[:, :], 31, 5, ALU.bitwise_and, ALU.logical_shift_left))
            done(v.tensor_scalar(e_tm2[:, :], e_dst[:, :], 11, None, ALU.arith_shift_right))
            done(v.tensor_tensor(e_tm3[:, :], e_tmp[:, :], e_tm2[:, :], ALU.bitwise_or))
            done(v.tensor_copy(part[1][:, :], e_tm3[:, :]))
            done(v.tensor_scalar(e_tmp[:, :], e_dst[:, :], 2047, None, ALU.bitwise_and))
            done(v.tensor_scalar(part[2][:, :], e_tmp[:, :], 1.0, None, ALU.add))
            done(v.tensor_copy(part[3][:, :], e_typ[:, :]))
            for k, e in enumerate((e_src, e_dst)):
                done(v.tensor_scalar(e_tmp[:, :], e[:, :], 9, None, ALU.arith_shift_right))
                done(v.tensor_copy(key[k][:, :], e_tmp[:, :]))

            def invert_counts(c, b):
                done(v.tensor_scalar(st[b][:, 5, :], block_of(T, c)[:, :, D:W].rearrange("p t w -> p (t w)"), 1.0, None, ALU.max))
                v.reciprocal(st[b][:, 6, :], st[b][:, 5, :]).then_inc(counts_inverted, 1)

            def norms(second):
                base = NB if second else 0
                X = x1b if second else xb
                centred_in = (cen, cen) if second else (cen, x1b[0])

                def mean(b):
                    done(v.tensor_reduce(st[b][:, 0, :], X[b][:, :, :], AX.X, ALU.add))
                    return begun(v.tensor_scalar(st[b][:, 1, :], st[b][:, 0, :], 1.0 / D, None, ALU.mult))

                def centre(b, begun_mean):
                    dve.wait_ge(vdone, begun_mean)
                    v.tensor_tensor(centred_in[b][:, :, :], X[b][:, :, :],
                                    st[b][:, 1, :].rearrange("p (t o) -> p t o", o=1).broadcast_to([P, BT, D]),
                                    ALU.subtract).then_inc(centred, 1)

                def scale(c, b, uses):
                    o = 1 - b
                    dve.wait_ge(dev_ready, base + c)
                    inverse = begun(v.reciprocal(st[o][:, 4, :], st[o][:, 3, :]))
                    wait(dve, h16_stored[o] if second else hb_stored[o], (uses - 1 + b) * 16)
                    if second and within(c - 3):
                        dve.wait_ge(h1_turned, c - 2)
                    dve.wait_ge(vdone, inverse)
                    v.scalar_tensor_tensor(
                        out=hb[o][:, :, :], in0=centred_in[o][:, :, :], scalar=0.0,
                        in1=st[o][:, 4, :].rearrange("p (t o) -> p t o", o=1).broadcast_to([P, BT, D]),
                        op0=ALU.max, op1=ALU.mult).then_inc(hb_ready[o], 1)

                def body(c, b, uses):
                    o = 1 - b
                    if within(c):
                        dve.wait_ge(x_loaded[b], moved(name_of(c), uses) + (moved_pass(b) if second else 0))
                        if second:
                            wait(dve, x1_stored[b], uses * 16)
                            dve.wait_ge(pooled_ready, c + 1)
                            v.tensor_tensor(x1b[b][:, :, :], xb[b][:, :, :], pooled, ALU.add).then_inc(x1_ready, 1)
                        else:
                            begun_mean = mean(b)
                    if within(c - 1):
                        dve.wait_ge(squared, base + c)
                        v.tensor_reduce(st[o][:, 2, :], sq[:, :, :], AX.X, ALU.add).then_inc(var_ready, 1)
                    if within(c) and second:
                        dve.wait_ge(x1_ready, c + 1)
                        begun_mean = mean(b)
                    if within(c) and not second:
                        if within(c - 2):
                            dve.wait_ge(hb_ready[b], uses)
                        centre(b, begun_mean)
                    if within(c - 1):
                        scale(c, b, uses)
                    if second and within(c + 1):
                        invert_counts(c + 1, o)
                    if second and within(c):
                        if within(c - 1):
                            dve.wait_ge(hb_ready[o], PAIRS + 1 - o + uses + b)
                        centre(b, begun_mean)
                    if second and within(c - 1):
                        dve.wait_ge(hb_ready[o], PAIRS + 1 - o + uses + b)
                        v.tensor_copy(h16[o][:, :, 3 * D:4 * D], hb[o][:, :, :]).then_inc(hi16_twice, 1)

                per = 4 if second else 3
                for c in range(4):
                    body(c, c % 2, c // 2)
                loop_starts()
                with dve.Fori(2, PAIRS - 1) as i:
                    for b in range(2):
                        turn((i - 2) * 2 + b, per)
                        body(i * 2 + b, b, i)
                loop_ends(2 * PAIRS - 6, per)
                for c in range(2 * PAIRS - 2, NB + 1):
                    body(c, c % 2, c // 2)

            norms(False)
            for b in range(2):
                dve.wait_ge(hb_stored[b], moved_pass(b))

            def over_unsorted(body):
                for b in range(2):
                    body(b, b)
                with dve.Fori(1, SG // 2) as i:
                    for b in range(2):
                        body(i * 2 + b, b)

            def hots(out_, k, t):
                return v.tensor_tensor(
                    out_.rearrange("p (u g) -> p u g", u=TG),
                    iota16[0:EP, 0:NG].rearrange("p (o g) -> p o g", o=1).broadcast_to([EP, TG, NG]),
                    key[k][:, ds(t * TG, TG)].rearrange("p (u o) -> p u o", o=1).broadcast_to([EP, TG, NG]),
                    ALU.is_equal)

            def source_hots(t):
                hots(kept_hot[:, ds(t * (TG * NG), TG * NG)], 0, t).then_inc(kept_ready, 1)

            def destination_hots(t, b, i):
                dve.wait_ge(key_used[b], i)
                hots(key_hot[b][:, :], 1, t).then_inc(key_ready, 1)

            for b in range(2):
                dve.sem_inc(key_used[b], 1)
            def over_unsorted(body):
                for t in range(4):
                    body(t, t % 2, t // 2)
                with dve.Fori(1, SG // 4) as j:
                    for c in range(4):
                        body(j * 4 + c, c % 2, j * 2 + c // 2)

            def both_hots(t, b, i):
                source_hots(t)
                destination_hots(t, b, i + 1)
            over_unsorted(both_hots)
            for s in range(2):
                dve.wait_ge(counted, s + 1)
                done(v.tensor_copy(totals[:, :], (p_run, p_tr)[s][:, 0:NG]))
                done(v.tensor_tensor_scan(starts[:, :], ones32[:, 0:NG], totals[:, :], 0.0, ALU.mult, ALU.add))
                v.tensor_tensor(starts[:, :], starts[:, :], totals[:, :], ALU.subtract).then_inc(starts_ready, 1)

            def places(s, t, hots):
                dve.wait_ge(ranks_ready[s], t + 1)
                if not isinstance(t, int) or t > 0:
                    dve.wait_ge(ranks_read[s], t)
                for u in range(TG):
                    m = v.scalar_tensor_tensor(out=junk[:, s * TG + u, :], in0=(p_run, p_tr)[s][0:EP, u * NG:(u + 1) * NG],
                                               scalar=1.0, in1=hots(u), op0=ALU.mult, op1=ALU.mult,
                                               accum_out=pos_f[s][:, ds(t * TG + u, 1)])
                m.then_inc(ranks_read[s], 1)

            def ranked(t, b, i):
                destination_hots(t, b, SG // 2 + i + 1)
                if not isinstance(t, int) or t > 0:
                    places(1, t - 1, lambda u: key_hot[1 - b][:, u * NG:(u + 1) * NG])
                places(0, t, lambda u: kept_hot[:, ds(t * (TG * NG) + u * NG, NG)])
            dve.wait_ge(key_ready, SG)
            over_unsorted(ranked)
            places(1, SG - 1, lambda u: key_hot[1][:, u * NG:(u + 1) * NG])

            def sort(s):
                dve.wait_ge(ranks_read[s], SG)
                done(v.tensor_copy(e_tmp[:, :], pos_f[s][:, :]))
                done(v.tensor_scalar(e_tm2[:, :], e_tmp[:, :], 7, None, ALU.arith_shift_right))
                done(v.tensor_scalar(e_tm3[:, :], e_tmp[:, :], P - 1, None, ALU.bitwise_and))
                done(v.tensor_copy(place_hi[:, :], e_tm2[:, :]))
                done(v.tensor_copy(place_lo[:, :], e_tm3[:, :]))
                with dve.Fori(0, ET // PB) as i:
                    for b in range(PB):
                        t = i * PB + b
                        dve.wait_ge(place_used, s * ET + t + 1)
                        v.tensor_scalar(eq_hot[b][:, :], iota16[0:EP, 0:P], place_lo[:, ds(t, 1)], None,
                                        ALU.is_equal).then_inc(eq_ready, 1)
                        m = v.tensor_scalar(hi_hot[b][:, :], iota16[0:EP, :], place_hi[:, ds(t, 1)], None, ALU.is_equal)
                        if s or act_pieces(s, b) == 1:
                            c = 3 if s else 1
                            m = v.tensor_scalar(lo_hot[b][:, c, :], iota16[0:EP, 0:P], place_lo[:, ds(t, 1)],
                                                part[c][:, ds(t, 1)], ALU.is_equal, ALU.mult)
                        m.then_inc(place_ready, 1)
                dve.wait_ge(place_used, (s + 1) * ET + PB)
                done(v.tensor_copy(dec_i[0][:, :], pk[1][:, 0:NT]))
                done(v.tensor_scalar(dec_i[1][:, :], dec_i[0][:, :], 5, None, ALU.arith_shift_right))
                done(v.tensor_copy(dec[0][:, :], dec_i[1][:, :]))
                done(v.scalar_tensor_tensor(out=dec[1][:, :], in0=pk[0][:, 0:NT], scalar=32.0, in1=dec[0][:, :],
                                            op0=ALU.mult, op1=ALU.add))
                done(v.tensor_copy(srt_src[s][:, 0:NT], dec[1][:, :]))
                done(v.tensor_scalar(dec_i[1][:, :], dec_i[0][:, :], 31, None, ALU.bitwise_and))
                done(v.tensor_copy(dec[0][:, :], dec_i[1][:, :]))
                done(v.tensor_scalar(dec[2][:, :], pk[2][:, 0:NT], -1.0, 0.0, ALU.add, ALU.max))
                done(v.scalar_tensor_tensor(out=dec[2][:, :], in0=dec[0][:, :], scalar=2048.0, in1=dec[2][:, :],
                                            op0=ALU.mult, op1=ALU.add))
                if s == 0:
                    done(v.tensor_copy(srt_dst[:, 0:NT], dec[2][:, :]))
                else:
                    done(v.tensor_copy(srt_typ[:, :], pk[3][:, 0:NT]))
                seg = dec[1] if s == 0 else dec[2]
                done(v.tensor_copy(dec_i[0][0:1, :], seg[0:1, :]))
                done(v.tensor_scalar(dec_i[1][0:1, :], dec_i[0][0:1, :], 9, None, ALU.arith_shift_right))
                done(v.tensor_copy(first_group[s][0:1, 0:ES],
                                   dec_i[1][0:1, :].rearrange("p (s u) -> p s u", u=TG)[:, :, 0]))
                done(v.memset(first_group[s][0:1, 0:1], 0))
                done(v.memset(first_group[s][0:1, ES:ES + 1], NG - 1))
                done(v.tensor_scalar(dec[0][:, :], pk[2][:, 0:NT], 0.0, -65536.0, ALU.is_equal, ALU.mult))
                v.tensor_tensor(node[s][:, :], seg[:, :], dec[0][:, :], ALU.add).then_inc(pieces_read, 1)
                dve.wait_ge(pieces_read, s + 1)

            def put_idx(layer, s, b):
                m = v.tensor_copy(idx[b][:, 0, :], srt_src[layer][:, ds(s * TG, TG)])
                if layer == 0:
                    m = v.tensor_copy(idx[b][:, 1, :], srt_dst[:, ds(s * TG, TG)])
                m.then_inc(idx_ready[b], 1)

            dve.sem_inc(place_used, PB)
            sort(0)
            for b in range(2):
                put_idx(0, b, b)
            sort(1)
            dve.sem_inc(sorted_ready, 1)

            def add_step(sums, g):
                dve.wait_ge(hot_used, sums)
                tg = T[:, ds(g, 1), :, :].rearrange("p g r w -> p (g r w)")
                v.tensor_tensor(tg, tg, p_run[:, 0:R * W], ALU.add).then_inc(step_added, 1)

            def steps(layer, s):
                g0, g1 = groups_of(mybir.EngineType.DVE, layer, s)
                with dve.Fori(g0, g1 + 1) as g:
                    k = s + g + layer * STEPS
                    used = dve.snap(k * TG)
                    summed = dve.snap(used + TG)
                    before = dve.snap((g - ((g - g0 + 127) >> 7)).with_bounds(min_val=0, max_val=NG - 1))
                    dve.wait_ge(hot_used, used + 1)
                    for u in range(TG):
                        v.tensor_scalar(hot[u][:, :, :].rearrange("p r n -> p (r n)"), iota512[:, :],
                                        group_base[:, ds(g, 1)], node[layer][:, ds(s * TG + u, 1)],
                                        ALU.add, ALU.is_equal).then_inc(hot_ready, 1)
                        if u == 0:
                            add_step(summed, before)

            def last_step(layer):
                add_step(((layer + 1) * STEPS + 1) * TG, NG - 1)

            def next_idx(layer, s, b, i):
                if has(s, 2):
                    per = 32 * TG if layer == 0 else 16 * TG
                    dve.wait_ge(gathered[b], layer * 16 * TG * ES + per * (i + 2))
                    if has(s, 4):
                        put_idx(layer, s + 4, b)
                    elif layer == 0:
                        put_idx(1, s + 4 - ES, b)

            def parts(layer, s, b, between=lambda: None):
                n = layer * ES + s
                dve.wait_ge(hi_ready, n + 1)
                v.tensor_tensor(mrest[:, :, :], msum[:, :, :], msg_hi[b][:, :, 0:D], ALU.subtract).then_inc(rest_ready, 1)
                between()
                dve.wait_ge(mid_ready, n + 1)
                v.tensor_tensor(msg_lo[b][:, :, :], mrest[:, :, :], msg_mid[b][:, :, :], ALU.subtract).then_inc(msg_ready, 1)

            dve.sem_inc(hot_used, TG)
            def message(s):
                dve.wait_ge(gate_ready, s + 1)
                v.scalar_tensor_tensor(out=msum[:, :, :], in0=gate[:, :, :], scalar=1.0,
                                       in1=p_out[:, :].rearrange("p (u e f) -> p u e f", u=TG, e=2)[:, :, 0, :],
                                       op0=ALU.add, op1=ALU.mult).then_inc(msum_ready, 1)

            def layer0(s, b, i):
                steps(0, s)
                next_idx(0, s, b, i)
                if has(s, 1):
                    message(s + 1)
                    parts(0, s + 1, 1 - b)
            for b in range(2):
                next_idx(0, b - 2, b, -1)
            message(0)
            parts(0, 0, 0)
            dve.wait_ge(step_cleared, 1)
            dve.wait_ge(table_cleared, 2)
            over_sets(dve, layer0)
            last_step(0)

            dve.wait_ge(step_added, STEPS + 2)
            invert_counts(0, 0)
            norms(True)
            dve.wait_ge(loop_added, NB)

            def relations(s, tiles):
                wait(dve, rel_turned, s)
                for u in tiles:
                    m = v.tensor_scalar(rel_hot[:, u, :], rel3[:, :], srt_typ[:, ds(s * TG + u, 1)], None, ALU.is_equal)
                m.then_inc(rel_ready, 1)

            def message1(s):
                dve.wait_ge(quarter_ready, s + 1)
                dve.wait_ge(msg_ready, ES + s)
                v.tensor_tensor(msum[:, :, :], quarter[:, :, 0, :], quarter[:, :, 1, :], ALU.add).then_inc(msum_ready, 1)

            def weigh(s, b):
                dve.wait_ge(cof_ready, s + 1)
                wait(dve, half_ready, 2 * s)
                for u in range(TG):
                    dve.wait_ge(edge_ready, s * TG + u + 1)
                    v.tensor_tensor(weighed[:, u, :, :], pk[u][:, :].rearrange("p (b f) -> p b f", b=BASES),
                                    cof[b][:, u, :].rearrange("p (b o) -> p b o", o=1).broadcast_to([P, BASES, D]),
                                    ALU.mult).then_inc(weighed_ready, 1)

            def layer1(s, b, i):
                if has(s, 1):
                    weigh(s + 1, 1 - b)
                steps(1, s)
                next_idx(1, s, b, i)
                if has(s, 1):
                    message1(s + 1)
                if has(s, 3):
                    relations(s + 3, (0, 1))
                if has(s, 1):
                    parts(1, s + 1, 1 - b, lambda: relations(s + 3, (2, 3)) if has(s, 3) else None)
            for s in range(3):
                relations(s, (0, 1))
                relations(s, (2, 3))
            for b in range(2):
                next_idx(1, b - 2, b, -1)
            weigh(0, 0)
            message1(0)
            parts(1, 0, 0)
            dve.wait_ge(step_cleared, 2)
            over_sets(dve, layer1)
            last_step(1)
            dve.wait_ge(step_added, 2 * STEPS + 3)

            def third(q, b, uses):
                dve.wait_ge(x1_loaded[b], (uses + (2 if name_of(q) is None else 1)) * 16)
                wait(dve, out_stored[b], uses * 16)
                v.scalar_tensor_tensor(out=out_of[b][:, :, :], in0=block_of(T, q)[:, :, 0:D], scalar=0.0,
                                       in1=x1_in[b][:, :, :], op0=ALU.max, op1=ALU.add).then_inc(out_ready, 1)
            over_fours(third, dve)


_INS = ['x', 'src', 'dst', 'edge_type_32', 'L0_gnn_W1', 'L0_gnn_b1', 'L0_gnn_W2', 'L0_gnn_b2', 'L0_gnn_Wg', 'L0_gnn_bg',
        'L1_gnn_coeff', 'L1_gnn_W', 'L1_gnn_h_bias', 'L1_gnn_loop_weight']


def kernel(**inputs):
    import numpy as _np
    import concourse.bacc as _bacc
    from concourse import mybir as _mybir
    from concourse.bass_utils import run_bass_kernel_spmd as _run

    nc = _bacc.Bacc("TRN2", target_bir_lowering=False, num_devices=1)
    arrays, args = {}, []
    for name in _INS:
        a = _np.ascontiguousarray(inputs[name])
        arrays[f"in_{name}"] = a
        args.append(nc.dram_tensor(f"in_{name}", a.shape, _mybir.dt.from_np(a.dtype), kind="ExternalInput").ap())
    args.append(nc.dram_tensor("out_0", (N, D), F32, kind="ExternalOutput").ap())
    gnn_kernel(nc, *args)
    r = _run(nc, [arrays], core_ids=[0])
    return r.results[0]["out_0"]
```
